# Optimizing a Trainium2 kernel written in Bass

```python
import numpy as np
import jax
import jax.numpy as jnp

def _softmax(x, axis=-1):
    return jax.nn.softmax(x, axis=axis)

def _gelu(x):
    return jax.nn.gelu(x, approximate=True)

def _silu(x):
    return jax.nn.silu(x)

def _sigmoid(x):
    return jax.nn.sigmoid(x)

def _layernorm(x, axis=-1, eps=1e-05):
    m = jnp.mean(x, axis=axis, keepdims=True)
    v = jnp.var(x, axis=axis, keepdims=True)
    return (x - m) / jnp.sqrt(v + eps)

def _scatter_add(tgt, idx, src, axis=0):
    return tgt.at[idx].add(src)

def _segment_sum(src, seg, n):
    return jax.ops.segment_sum(src, seg, n)
kernel_name = 'mk_adj_preln_d2_adj_r2_c76716'

def setup_inputs(seed: int=0):
    np.random.seed(seed)
    _w = jnp.asarray

    def _rec_inputs():
        import jax
        import jax.numpy as jnp
        _gk = jax.random.key(seed)
        x = -0.000929 + 1 * jax.random.normal(jax.random.fold_in(_gk, 1), (4096, 128), jnp.float32)
        _a = jax.random.bernoulli(jax.random.fold_in(_gk, 2), 0.00195312, (4096, 4096))
        _a = jnp.logical_or(_a, jnp.swapaxes(_a, -1, -2))
        _a = jnp.logical_or(_a, jnp.eye(4096, dtype=bool))
        adj = _a.astype(jnp.int32)
        return (x, adj)
    x, adj = _rec_inputs()

    def _L0_gnn_setup():
        import jax, jax.numpy as jnp
        import numpy as np
        from jax import lax
        N = 4096
        D = 128
        CHUNK = 128
        key = jax.random.key(seed)
        k1, k2 = jax.random.split(key)
        x = jax.random.normal(k1, (N, D), dtype=jnp.float32)
        adj = jax.random.randint(k2, (N, N), 0, 2, dtype=jnp.int32)
        return {'x': x, 'adj': adj}
    _L0_gnn_all = _L0_gnn_setup()
    _L0_gnn_in = {k: v for k, v in _L0_gnn_all.items() if k in ()}
    del _L0_gnn_all

    def _L1_gnn_setup():
        import jax, jax.numpy as jnp
        import numpy as np
        N = 4096
        D_IN = 128
        D_OUT = 128
        ALPHA = 0.2
        NEG = -9000000000000000.0
        key = jax.random.key(seed)
        k1, k2, k3, k4 = jax.random.split(key, 4)
        input = jax.random.normal(k1, (N, D_IN), dtype=jnp.float32)
        adj = jax.random.randint(k2, (N, N), 0, 2, dtype=jnp.int32)
        lim_w = 1.414 * np.sqrt(6.0 / (D_IN + D_OUT))
        W = jax.random.uniform(k3, (D_IN, D_OUT), jnp.float32, -lim_w, lim_w)
        lim_a = 1.414 * np.sqrt(6.0 / (2 * D_OUT + 1))
        a = jax.random.uniform(k4, (2 * D_OUT, 1), jnp.float32, -lim_a, lim_a)
        return {'input': input, 'adj': adj, 'W': W, 'a': a}
    _L1_gnn_all = _L1_gnn_setup()
    _L1_gnn_in = {k: v for k, v in _L1_gnn_all.items() if k in ('W', 'a')}
    del _L1_gnn_all
    return {'x': x, 'adj': adj, 'L1_gnn_W': _L1_gnn_in['W'], 'L1_gnn_a': _L1_gnn_in['a']}

def reference(x, adj, L1_gnn_W, L1_gnn_a):
    import jax
    import jax.numpy as jnp

    def _L0_gnn_ref(x, adj):
        import jax, jax.numpy as jnp
        import numpy as np
        from jax import lax
        N = 4096
        D = 128
        CHUNK = 128
        n, d = x.shape
        neg = jnp.finfo(x.dtype).min
        adj_chunks = adj.reshape(n // CHUNK, CHUNK, n)

        def step(carry, a):
            mask = a != 0
            masked = jnp.where(mask[:, :, None], x[None, :, :], neg)
            m = jnp.max(masked, axis=1)
            has_nbr = jnp.any(mask, axis=1)
            out = jnp.where(has_nbr[:, None], m, jnp.zeros((), x.dtype))
            return (carry, out)
        _, out = lax.scan(step, None, adj_chunks)
        return out.reshape(n, d)

    def _L1_gnn_ref(input, adj, W, a):
        import jax, jax.numpy as jnp
        import numpy as np
        N = 4096
        D_IN = 128
        D_OUT = 128
        ALPHA = 0.2
        NEG = -9000000000000000.0
        h = input @ W
        a1 = a[:D_OUT, 0]
        a2 = a[D_OUT:, 0]
        e = (h @ a1)[:, None] + (h @ a2)[None, :]
        e = jnp.where(e > 0, e, ALPHA * e)
        e = jnp.where(adj > 0, e, NEG)
        attention = jax.nn.softmax(e, axis=1)
        h_prime = attention @ h
        return jax.nn.elu(h_prime)
    h = jnp.maximum(_layernorm(x, axis=-1), 0.0)
    x = x + _L0_gnn_ref(h, adj)
    h = jnp.maximum(_layernorm(x, axis=-1), 0.0)
    x = x + _L1_gnn_ref(h, adj, L1_gnn_W, L1_gnn_a)
    return x

_drawn_inputs = setup_inputs


def setup_inputs(seed=0):
    import zlib

    import numpy as np

    out = dict(_drawn_inputs(seed))
    spreads = {}
    factors = {}
    for name, (base, spread) in spreads.items():
        noise = np.random.default_rng([zlib.crc32(name.encode()), seed]).standard_normal(out[name].shape)
        drawn = base * np.exp(spread * noise) if base else spread * noise
        out[name] = jnp.asarray(drawn.astype(out[name].dtype))
    for name, factor in factors.items():
        out[name] = (out[name] * factor).astype(out[name].dtype)
    return out
```

```python
import concourse.bass as bass
from concourse import mybir
from contextlib import ExitStack

F32, F16, BF16, I32 = mybir.dt.float32, mybir.dt.float16, mybir.dt.bfloat16, mybir.dt.int32
ALU, ACT, AX = mybir.AluOpType, mybir.ActivationFunctionType, mybir.AxisListType

P = 128
N = 4096
D = 128
C = N // P
TI = 512
TILES = N // TI
ROWS = TI // P
PAIR = 2
STEPS = C // PAIR
UNIT = 4
UNITS = STEPS // UNIT
UCOLS = UNIT * PAIR * P
W = PAIR * TI
ROUNDS = 4
MARK = 1024.0
HSCALE = 4096.0
EPS = 1e-5
FAR = 2.0 ** 93
ALPHA = 0.2


def gnn_two_layers(nc, x, adj, w, a, out):
    ctx = ExitStack()
    with ctx:
        def sb(name, shape, dt, at=None):
            return (at or ctx).enter_context(nc.sbuf_tensor(name, shape, dt))

        def sem(name):
            return ctx.enter_context(nc.semaphore(name))

        ident_b = sb("ident_b", [P, P], BF16)
        ident32 = sb("ident32", [P, P], F32)
        order_w = sb("order_w", [P, P], F16)
        diff_i = sb("diff_i", [P, P], I32)
        diff = sb("diff", [P, P], F32)
        rank_i = sb("rank_i", [P, P], I32)
        rank_tab = sb("rank_tab", [P, P], F32)
        chunk_i = sb("chunk_i", [C, 1], I32)
        chunk_no = sb("chunk_no", [C, 1], F32)
        best = sb("best", [P, N], F32)

        x_rows = x.rearrange("(c p) d -> p c d", p=P)
        out_rows = out.rearrange("(c p) d -> p c d", p=P)

        absent_rows = nc.dram_tensor("absent_rows", (N, N), BF16).ap()

        with ExitStack() as layer0:
            h_hi = sb("h_hi", [P, C, D], F16, layer0)
            h_lo = sb("h_lo", [P, C, D], F16, layer0)
            prepare(nc, x_rows, h_hi, h_lo, ident_b, ident32, order_w, diff_i, diff, rank_i, rank_tab, chunk_i, chunk_no)
            neighbour_max(nc, adj, absent_rows, h_hi, h_lo, ident_b, order_w, rank_tab, chunk_no, best)
        with ExitStack() as layer1:
            x1 = sb("x1", [P, C, D], F32, layer1)
            wh = sb("wh", [P, C, D + 1], F32, layer1)
            score_t = sb("score_t", [P, N], F32, layer1)
            score_s = sb("score_s", [P, C], F32, layer1)
            project(nc, x_rows, w, a, ident32, best, x1, wh, score_t, score_s)
            attend(nc, absent_rows, out_rows, ident32, x1, wh, score_t, score_s)


def wait_apart(eng, sem, value, passed):
    eng.wait_ge(sem, value)
    eng.sem_inc(passed, 1)


def prepare(nc, x_rows, h_hi, h_lo, ident_b, ident32, order_w, diff_i, diff, rank_i, rank_tab, chunk_i, chunk_no):
    ctx = ExitStack()
    with ctx:
        xs = ctx.enter_context(nc.sbuf_tensor("xs", [P, C, D], F32))
        hs = ctx.enter_context(nc.sbuf_tensor("hs", [P, C, D], F32))
        stats = ctx.enter_context(nc.sbuf_tensor("ln1_stats", [P, C, 6], F32))
        mom = ctx.enter_context(nc.sbuf_tensor("ln1_mom", [P, C, 2], F32))
        std = ctx.enter_context(nc.sbuf_tensor("ln1_std", [P, C], F32))
        rstd = ctx.enter_context(nc.sbuf_tensor("ln1_rstd", [P, C], F32))
        eps = ctx.enter_context(nc.sbuf_tensor("ln1_eps", [P, 1], F32))
        sem = lambda name: ctx.enter_context(nc.semaphore(name))
        x_in = [sem(f"x_in{i}") for i in range(4)]
        iotas, consts, var_ready, std_ready, step = sem("iotas"), sem("consts"), sem("var_ready"), sem("std_ready"), sem("ln1_step")
        hs_ready, hi_ready = sem("hs_ready"), sem("hi_ready")
        G = C // 4
        with nc.Block() as block:
            @block.sync
            def _(sp):
                for i in range(4):
                    sp.dma_start(xs[:, i * G:(i + 1) * G, :], x_rows[:, i * G:(i + 1) * G, :]).then_inc(x_in[i], 16)

            @block.gpsimd
            def _(pool):
                pool.iota(diff_i[:, :], pattern=[[1, P]], base=0, channel_multiplier=-1).then_inc(iotas, 1)
                pool.iota(rank_i[:, :], pattern=[[1, P]], base=-int(MARK), channel_multiplier=0).then_inc(iotas, 1)
                pool.iota(chunk_i[:, :], pattern=[[1, 1]], base=0, channel_multiplier=1).then_inc(iotas, 1)

            @block.scalar
            def _(act):
                act.wait_ge(var_ready, 1)
                nc.scalar.activation(std[:, :], mom[:, :, 1], ACT.Sqrt, bias=eps[:, :]).then_inc(std_ready, 1)
                act.wait_ge(hs_ready, 1)
                nc.scalar.activation(h_hi[:, :, :], hs[:, :, :], ACT.Copy).then_inc(hi_ready, 1)

            @block.vector
            def _(dve):
                n = [0]

                def link(ins):
                    n[0] += 1
                    ins.then_inc(step, 1)
                    dve.wait_ge(step, n[0])

                nc.vector.memset(eps[:, :], EPS)
                dve.wait_ge(iotas, 3)
                nc.vector.tensor_copy(rank_tab[:, :], rank_i[:, :])
                nc.vector.tensor_copy(chunk_no[:, :], chunk_i[:, :])
                link(nc.vector.tensor_copy(diff[:, :], diff_i[:, :]))
                nc.vector.tensor_scalar(ident_b[:, :], diff[:, :], 0.0, None, ALU.is_equal)
                link(nc.vector.tensor_scalar(ident32[:, :], diff[:, :], 0.0, -MARK, ALU.is_equal, ALU.mult))
                link(nc.vector.scalar_tensor_tensor(out=order_w[:, :], in0=diff[:, :], scalar=0.0, in1=ident32[:, :],
                                                    op0=ALU.is_gt, op1=ALU.add))
                nc.vector.tensor_scalar(ident32[:, :], diff[:, :], 0.0, None, ALU.is_equal)
                for i in range(4):
                    dve.wait_ge(x_in[i], 16)
                    for c in range(i * G, (i + 1) * G):
                        last = nc.vector.bn_stats(stats[:, c, :], xs[:, c, :])
                link(last)
                for c in range(C):
                    last = nc.vector.bn_aggr(mom[:, c, :], stats[:, c, :])
                last.then_inc(var_ready, 1)
                dve.wait_ge(std_ready, 1)
                link(nc.vector.reciprocal(rstd[:, :], std[:, :]))
                link(nc.vector.tensor_tensor(std[:, :], rstd[:, :], rstd[:, :], ALU.mult))
                link(nc.vector.scalar_tensor_tensor(out=std[:, :], in0=mom[:, :, 1], scalar=eps[:, :], in1=std[:, :],
                                                    op0=ALU.add, op1=ALU.mult))
                link(nc.vector.tensor_scalar(std[:, :], std[:, :], -0.5, 1.5, ALU.mult, ALU.add))
                link(nc.vector.tensor_tensor(rstd[:, :], rstd[:, :], std[:, :], ALU.mult))
                for c in range(C):
                    last = nc.vector.tensor_scalar(hs[:, c, :], xs[:, c, :], mom[:, c, 0:1], rstd[:, c:c + 1],
                                                   ALU.subtract, ALU.mult)
                link(last)
                link(nc.vector.tensor_scalar(hs[:, :, :], hs[:, :, :], 0.0, HSCALE, ALU.max, ALU.mult))
                nc.vector.sem_inc(hs_ready, 1)
                dve.wait_ge(hi_ready, 1)
                nc.vector.tensor_tensor(h_lo[:, :, :], hs[:, :, :], h_hi[:, :, :], ALU.subtract)


def neighbour_max(nc, adj, absent_rows, h_hi, h_lo, ident_b, order_w, rank_tab, chunk_no, best):
    ctx = ExitStack()
    with ctx:
        sb = lambda name, shape, dt: ctx.enter_context(nc.sbuf_tensor(name, shape, dt))
        ps = lambda name, shape, dt: ctx.enter_context(nc.psum_tensor(name, shape, dt))
        sem = lambda name: ctx.enter_context(nc.semaphore(name))
        stage = sb("stage", [P, 2, ROWS, UCOLS], I32)
        absent = sb("absent", [P, 2, ROWS, UCOLS], BF16)
        edge_t = sb("edge_t", [P, W], F16)
        order = sb("order", [P, 2, C, TI], F16)
        sel0, sel1 = sb("sel0", [P, 2, W], F16), sb("sel1", [P, 2, W], F16)
        sel2, sel3 = sb("sel2", [P, W], F16), sb("sel3", [P, W], F16)
        acc = sb("acc", [P, 2, 2, W], F32)
        xsel = sb("xsel", [P, TI], F16)
        neg = sb("neg", [P, 1], F32)
        far = sb("far", [P, 1], F32)
        last_row = sb("last_row", [C, TI], F16)
        lr_flag = sb("lr_flag", [C, TI], F32)
        lr_cnt = sb("lr_cnt", [C, TI], F32)
        key_sq = sb("key_sq", [32, 32], F32)
        key_row = sb("key_row", [32, 32], F32)
        key_sorted = sb("key_sorted", [1, C], F32)
        key_int = sb("key_int", [1, C], I32)
        x_chunk = sb("x_chunk", [1, C], I32)
        x_deg = sb("x_deg", [1, C], I32)
        x_degf = sb("x_degf", [1, C], F32)
        x_extra = sb("x_extra", [1, C + 1], F32)
        x_scan = sb("x_scan", [1, C + 1], F32)
        zeros = sb("zeros", [1, C + 1], F32)
        x_has = sb("x_has", [1, C], F32)
        x_count = sb("x_count", [1, 1], F32)
        x_counti = sb("x_counti", [1, 1], I32)
        x_start = sb("x_start", [1, C + 1], I32)

        flip_ps = ps("flip_ps", [P, W], BF16)
        order_ps = ps("order_ps", [P, W], F32)
        pick_ps = [ps(f"pick_ps{i}", [P, W], F32) for i in range(2)]
        extra_ps = ps("extra_ps", [P, TI], F32)

        landed = [sem(f"landed{i}") for i in range(2)]
        kept = [sem(f"kept{i}") for i in range(2)]
        absent_free = sem("absent_free")
        mask_ready = sem("mask_ready")
        flipped = sem("flipped")
        edge_ready = sem("edge_ready")
        ordered = sem("ordered")
        sel0_ready = sem("sel0_ready")
        order_ready = sem("order_ready")
        sel1_ready = sem("sel1_ready")
        sel_ready = sem("sel_ready")
        picked = sem("picked")
        pick_free = sem("pick_free")
        row_in = sem("row_in")
        row_free = sem("row_free")
        plan_ready = sem("plan_ready")
        plan_read = sem("plan_read")
        extras_done = sem("extras_done")
        xsel_ready = sem("xsel_ready")
        xpicked = sem("xpicked")
        xkept = sem("xkept")
        step = sem("l0_step")
        passed_pool, passed_pe, passed_dve, passed_sp = (sem("passed_" + e) for e in ("pool", "pe", "dve", "sp"))
        neg_ready = sem("neg_ready")

        def order_of(b, p):
            return order[:, b, p * PAIR:(p + 1) * PAIR, :].rearrange("p c i -> p (c i)")

        def load_unit(sp, q, u, slot):
            sp.dma_start(stage[:, slot, :, :],
                         adj[bass.ds(q * TI, TI), u * UCOLS:(u + 1) * UCOLS].rearrange("(r p) j -> p r j", p=P)
                         ).then_inc(landed[slot], 16)

        def keep_unit(sp, q, u):
            sp.dma_start(absent_rows[bass.ds(q * TI, TI), u * UCOLS:(u + 1) * UCOLS].rearrange("(r p) j -> p r j", p=P),
                         absent[:, u % 2, :, :]).then_inc(kept[u % 2], 16)

        with nc.Block() as block:
            @block.sync
            def _(sp):
                sp.sem_inc(absent_free, 2)
                load_unit(sp, 0, 0, 0)
                load_unit(sp, 0, 1, 1)

                def tile(q, b, last):
                    for u in range(UNITS):
                        wait_apart(sp, mask_ready, (q * UNITS + u + 1) * UNIT, passed_sp)
                        keep_unit(sp, q, u)
                        if not (last and u + 2 >= UNITS):
                            load_unit(sp, q + (u + 2) // UNITS, (u + 2) % UNITS, u % 2)
                        wait_apart(sp, kept[u % 2], 16 * (q * (UNITS // 2) + u // 2 + 1), passed_sp)
                        sp.sem_inc(absent_free, 1)
                    wait_apart(sp, order_ready, q * STEPS + STEPS, passed_sp)
                    wait_apart(sp, row_free, q + 1, passed_sp)
                    sp.dma_start(last_row[:, :], order[P - 1:P, b, :, :]).then_inc(row_in, 16)

                with sp.Fori(0, TILES // 2 - 1) as qq:
                    for b in range(2):
                        tile(qq * 2 + b, b, False)
                for b in range(2):
                    tile(TILES - 2 + b, b, b == 1)
            @block.gpsimd
            def _(pool):
                def tile(q, b):
                    for p in range(STEPS):
                        wait_apart(pool, order_ready, q * STEPS + p + 1, passed_pool)
                        nc.gpsimd.tensor_scalar(sel1[:, p % 2, :], order_of(b, p), 1 - MARK, None, ALU.is_equal).then_inc(sel1_ready, 1)

                with pool.Fori(0, TILES // 2) as qq:
                    for b in range(2):
                        tile(qq * 2 + b, b)

            @block.scalar
            def _(act):
                def convert(u, s):
                    nc.scalar.activation(absent[:, u % 2, :, s * PAIR * P:(s + 1) * PAIR * P],
                                         stage[:, u % 2, :, s * PAIR * P:(s + 1) * PAIR * P],
                                         ACT.Relu, scale=-FAR, bias=far[:, :]).then_inc(mask_ready, 1)

                def edges(g):
                    act.wait_ge(flipped, g + 1)
                    nc.scalar.activation(edge_t[:, :], flip_ps[:, :], ACT.Relu, scale=-1.0, bias=1.0).then_inc(edge_ready, 1)

                def keep_order(g, b, p):
                    act.wait_ge(ordered, g + 1)
                    nc.scalar.activation(sel0[:, p % 2, :], order_ps[:, :], ACT.Relu, scale=-1.0, bias=neg[:, :]).then_inc(sel0_ready, 1)
                    nc.scalar.activation(order_of(b, p), order_ps[:, :], ACT.Copy).then_inc(order_ready, 1)

                def tile(q, b, last):
                    for p in range(STEPS):
                        g, u, s = q * STEPS + p, p // UNIT, p % UNIT
                        if p == STEPS - 1 and not last:
                            act.wait_ge(extras_done, q + 1)
                        if not (last and p == STEPS - 1):
                            keep_order(g + 1, (b + (p + 1) // STEPS) % 2, (p + 1) % STEPS)
                        if not (last and p >= STEPS - 2):
                            edges(g + 2)
                        if not (last and u == UNITS - 1):
                            if s == 0:
                                act.wait_ge(landed[(u + 1) % 2], 16 * (2 * q + (u + 1) // 2 + 1))
                                act.wait_ge(absent_free, q * UNITS + u + 2)
                            convert(u + 1, s)

                act.wait_ge(neg_ready, 2)
                act.wait_ge(landed[0], 16)
                for s in range(UNIT):
                    convert(0, s)
                edges(0)
                keep_order(0, 0, 0)
                edges(1)
                with act.Fori(0, TILES // 2 - 1) as qq:
                    for b in range(2):
                        tile(qq * 2 + b, b, False)
                for b in range(2):
                    tile(TILES - 2 + b, b, b == 1)

            @block.tensor
            def _(pe):
                def flip(g, p):
                    u, s = p // UNIT, p % UNIT
                    pe.wait_ge(mask_ready, g + 1)
                    for c in range(PAIR):
                        for r in range(ROWS):
                            last = nc.tensor.transpose(flip_ps[:, c * TI + r * P:c * TI + (r + 1) * P],
                                                       absent[:, u % 2, r, (s * PAIR + c) * P:(s * PAIR + c + 1) * P],
                                                       ident_b[:, :])
                    last.then_inc(flipped, 1)

                def rank(g):
                    pe.wait_ge(edge_ready, g + 1)
                    pe.wait_ge(order_ready, g)
                    for c in range(PAIR):
                        last = nc.tensor.matmul(order_ps[:, c * TI:(c + 1) * TI], order_w[:, :], edge_t[:, c * TI:(c + 1) * TI],
                                                start=True, stop=True)
                    last.then_inc(ordered, 1)

                def pick(g, p, k):
                    if k == 0:
                        pe.wait_ge(sel0_ready, g + 1)
                    elif k == 1:
                        pe.wait_ge(sel1_ready, g + 1)
                    else:
                        pe.wait_ge(sel_ready, g * (ROUNDS - 2) + k - 1)
                    pe.wait_ge(pick_free, g * ROUNDS + k + 1)
                    s = (sel0[:, p % 2, :], sel1[:, p % 2, :], sel2, sel3)[k]
                    dst = pick_ps[k % 2]
                    for c in range(PAIR):
                        for part, h in enumerate((h_hi, h_lo)):
                            last = nc.tensor.matmul(dst[:, c * TI:(c + 1) * TI], h[:, p * PAIR + c, :], s[:, c * TI:(c + 1) * TI],
                                                    start=part == 0, stop=part == 1)
                    last.then_inc(picked, 1)

                def extras(q):
                    wait_apart(pe, plan_ready, q + 1, passed_pe)
                    count = pe.value_load(x_counti[0:1, 0:1], min_val=0, max_val=C)
                    with pe.If(count > 0):
                        with pe.Fori(0, count) as e:
                            c = pe.value_load(x_chunk[0:1, bass.ds(e, 1)], min_val=0, max_val=C - 1)
                            deg = pe.value_load(x_deg[0:1, bass.ds(e, 1)], min_val=ROUNDS + 1, max_val=P)
                            start = pe.value_load(x_start[0:1, bass.ds(e, 1)], min_val=0, max_val=C * TILES * P)
                            with pe.Fori(ROUNDS, deg) as k:
                                pe.wait_ge(xsel_ready, start + k - ROUNDS + 1)
                                for part, h in enumerate((h_hi, h_lo)):
                                    last = nc.tensor.matmul(extra_ps[:, :], h[:, bass.ds(c, 1), :].rearrange("p c d -> p (c d)"),
                                                            xsel[:, :], start=part == 0, stop=part == 1)
                                last.then_inc(xpicked, 1)
                    pe.end_ifs()
                    pe.sem_inc(plan_read, 1)

                def tile(q, last):
                    for p in range(STEPS):
                        g = q * STEPS + p
                        if not (last and p == STEPS - 1):
                            rank(g + 1)
                        if not (last and p >= STEPS - 2):
                            flip(g + 2, (p + 2) % STEPS)
                        for k in range(ROUNDS):
                            pick(g, p, k)
                        if p == STEPS // 2 - 1:
                            extras(q)

                pe.sem_inc(plan_read, 1)
                flip(0, 0)
                rank(0)
                flip(1, 1)
                with pe.Fori(0, TILES - 1) as q:
                    tile(q, False)
                tile(TILES - 1, True)
                extras(TILES)

            @block.vector
            def _(dve):
                n = [0]

                def link(ins, at=None):
                    n[0] += 1
                    ins.then_inc(step, 1)
                    wait_apart(dve, step, n[0] if at is None else at + n[0], passed_dve)

                nc.vector.memset(far[:, :], FAR).then_inc(neg_ready, 1)
                nc.vector.memset(neg[:, :], 1.0 - MARK).then_inc(neg_ready, 1)
                nc.vector.memset(last_row[:, :], 0.0)
                nc.vector.memset(x_scan[:, :], 0.0)
                nc.vector.memset(key_sq[:, :], 0.0)
                nc.vector.memset(zeros[:, :], 0.0)
                nc.vector.memset(x_extra[:, :], 0.0)
                nc.vector.memset(acc[:, :, :, :], 0.0)
                link(nc.vector.memset(best[:, :], 0.0))
                nc.vector.sem_inc(pick_free, 2)
                nc.vector.sem_inc(row_free, 1)
                nc.vector.sem_inc(xkept, 1)
                pre = n[0]

                def maxima(q, b, lo, hi):
                    with dve.Fori(lo, hi) as p:
                        dve.wait_ge(order_ready, q * STEPS + p + 1)
                        for k in range(2, ROUNDS):
                            nc.vector.tensor_scalar((sel2, sel3)[k - 2][:, :], order[:, b, bass.ds(p * PAIR, PAIR), :].rearrange("p c i -> p (c i)"),
                                                    k - MARK, None, ALU.is_equal).then_inc(sel_ready, 1)
                        for k in range(ROUNDS):
                            dve.wait_ge(picked, (q * STEPS + p) * ROUNDS + k + 1)
                            dve.wait_ge(pick_free, (q * STEPS + p) * ROUNDS + k + 1)
                            nc.vector.tensor_tensor(acc[:, b, k % 2, :], pick_ps[k % 2][:, :], acc[:, b, k % 2, :],
                                                    ALU.max).then_inc(pick_free, 1)

                PLAN = 15

                def plan(q):
                    n[0] = 0
                    base = q * (PLAN + 5) + pre
                    lk = lambda ins: link(ins, base)
                    if not isinstance(q, int) or q > 0:
                        dve.wait_ge(row_in, q * 16)
                    dve.wait_ge(plan_read, q + 1)
                    lk(nc.vector.tensor_scalar(lr_flag[:, :], last_row[:, :], 0.0, MARK + 1.0, ALU.is_lt, ALU.mult))
                    lk(nc.vector.tensor_tensor(lr_cnt[:, :], last_row[:, :], lr_flag[:, :], ALU.add))
                    lk(nc.vector.tensor_reduce(lr_flag[:, 0:1], lr_cnt[:, :], AX.X, ALU.max))
                    nc.vector.sem_inc(row_free, 1)
                    lk(nc.vector.scalar_tensor_tensor(out=key_sq[:, 0:1], in0=lr_flag[:, 0:1], scalar=float(C), in1=chunk_no[:, :],
                                                      op0=ALU.mult, op1=ALU.add))
                    lk(nc.vector.transpose(key_row[:, :], key_sq[:, :]))
                    for t in range(C // 8):
                        nxt = nc.vector.max(key_sorted[:, t * 8:(t + 1) * 8], key_row[0:1, :])
                        if t < C // 8 - 1:
                            lk(nxt)
                            lk(nc.vector.match_replace(out=key_row[0:1, :], in_to_replace=key_sorted[:, t * 8:(t + 1) * 8],
                                                       in_values=key_row[0:1, :], imm_value=-1.0))
                    lk(nxt)
                    lk(nc.vector.tensor_copy(key_int[:, :], key_sorted[:, :]))
                    nc.vector.tensor_scalar(x_chunk[:, :], key_int[:, :], C - 1, None, ALU.bitwise_and)
                    lk(nc.vector.tensor_scalar(x_deg[:, :], key_int[:, :], 5, None, ALU.logical_shift_right))
                    nc.vector.tensor_scalar(x_has[:, :], x_deg[:, :], ROUNDS + 0.5, 0.0, ALU.is_gt, ALU.add, accum_out=x_count[:, :])
                    nc.vector.tensor_scalar(x_extra[:, 1:C + 1], x_deg[:, :], float(ROUNDS), 0.0, ALU.subtract, ALU.max)
                    assert n[0] == PLAN - 1, n[0]
                    lk(nc.vector.tensor_copy(x_extra[:, 0:1], x_scan[:, C:C + 1]))
                    nc.vector.tensor_copy(x_counti[:, :], x_count[:, :])
                    lk(nc.vector.tensor_tensor_scan(x_scan[:, :], x_extra[:, :], zeros[:, :], 0.0, ALU.add, ALU.add))
                    lk(nc.vector.tensor_copy(x_start[:, :], x_scan[:, :]))
                    nc.vector.sem_inc(plan_ready, 1)

                def extras(q, b):
                    count = dve.value_load(x_counti[0:1, 0:1], min_val=0, max_val=C)
                    with dve.If(count > 0):
                        with dve.Fori(0, count) as e:
                            c = dve.value_load(x_chunk[0:1, bass.ds(e, 1)], min_val=0, max_val=C - 1)
                            deg = dve.value_load(x_deg[0:1, bass.ds(e, 1)], min_val=ROUNDS + 1, max_val=P)
                            start = dve.value_load(x_start[0:1, bass.ds(e, 1)], min_val=0, max_val=C * TILES * P)
                            with dve.Fori(ROUNDS, deg) as k:
                                dve.wait_ge(xkept, start + k - ROUNDS + 1)
                                nc.vector.tensor_scalar(xsel[:, :], order[:, b, bass.ds(c, 1), :].rearrange("p c i -> p (c i)"),
                                                        rank_tab[:, bass.ds(k, 1)], None, ALU.is_equal).then_inc(xsel_ready, 1)
                                dve.wait_ge(xpicked, start + k - ROUNDS + 1)
                                nc.vector.tensor_tensor(acc[:, b, 0, 0:TI], extra_ps[:, :], acc[:, b, 0, 0:TI],
                                                        ALU.max).then_inc(xkept, 1)
                    dve.end_ifs()
                    total = dve.value_load(x_start[0:1, C:C + 1], min_val=0, max_val=C * TILES * P)
                    dve.wait_ge(xkept, total + 1)
                    nc.vector.sem_inc(extras_done, 1)

                def finish(q, b):
                    base = (q + 1) * (PLAN + 5) + pre
                    lk = lambda ins: link(ins, base)
                    lk(nc.vector.tensor_tensor(acc[:, b, 0, :], acc[:, b, 0, :], acc[:, b, 1, :], ALU.max))
                    lk(nc.vector.tensor_tensor(best[:, bass.ds(q * TI, TI)], acc[:, b, 0, 0:TI], acc[:, b, 0, TI:W], ALU.max))
                    lk(nc.vector.memset(acc[:, b, :, :], 0.0))

                def tile(q, b, first):
                    maxima(q, b, 0, STEPS // 4)
                    plan(q)
                    maxima(q, b, STEPS // 4, STEPS // 2)
                    extras(q, 1 - b)
                    if first:
                        nc.vector.sem_inc(step, 3)
                    else:
                        finish(q - 1, 1 - b)
                    maxima(q, b, STEPS // 2, STEPS)

                for b in range(2):
                    tile(b, b, b == 0)
                with dve.Fori(1, TILES // 2) as qq:
                    for b in range(2):
                        tile(qq * 2 + b, b, False)
                plan(TILES)
                extras(TILES, 1)
                finish(TILES - 1, 1)


def project(nc, x_rows, w, a, ident32, best, x1, wh, score_t, score_s):
    ctx = ExitStack()
    with ctx:
        sb = lambda name, shape, dt: ctx.enter_context(nc.sbuf_tensor(name, shape, dt))
        sem = lambda name: ctx.enter_context(nc.semaphore(name))
        h = sb("h1", [P, C, D], F32)
        h_t = sb("h1_t", [P, N], F32)
        wh_t = sb("wh_t", [P, N], F32)
        w_sb = sb("w_sb", [P, D], F32)
        a1 = sb("a1", [P, 1], F32)
        a2 = sb("a2", [P, 1], F32)
        ones = sb("ones", [P, P], F32)
        a2_wide = sb("a2_wide", [P, P], F32)
        stats, mom = sb("ln2_stats", [P, C, 6], F32), sb("ln2_mom", [P, C, 2], F32)
        std, rstd, eps = sb("ln2_std", [P, C], F32), sb("ln2_rstd", [P, C], F32), sb("ln2_eps", [P, 1], F32)
        banks = [ctx.enter_context(nc.psum_tensor(f"bank{i}", [P, 512], F32)) for i in range(6)]
        s_ps = ctx.enter_context(nc.psum_tensor("s_ps", [P, C], F32))
        x_in, w_in = sem("x1_in"), sem("w_in")
        put = sem("put")
        took = sem("took")
        x1_made, eps_made, mom_made, std_made, h_made, step, s_put = (sem(n) for n in (
            "x1_made", "eps_made", "mom_made", "std_made", "h_made", "ln2_step", "s_put"))
        GR = C // 4
        group = lambda t, g: t[:, g * 512:(g + 1) * 512]
        with nc.Block() as block:
            @block.sync
            def _(sp):
                sp.dma_start(x1[:, :, :], x_rows).then_inc(x_in, 16)
                sp.dma_start(w_sb[:, :], w).then_inc(w_in, 16)
                sp.dma_start(a1[:, :], a[0:D, :]).then_inc(w_in, 16)
                sp.dma_start(a2[:, :], a[D:2 * D, :]).then_inc(w_in, 16)

            @block.tensor
            def _(pe):
                for g in range(GR):
                    if g >= 6:
                        pe.wait_ge(x1_made, g - 5)
                    for c in range(4):
                        last = nc.tensor.transpose(banks[g % 6][:, c * P:(c + 1) * P], best[:, (g * 4 + c) * P:(g * 4 + c + 1) * P], ident32[:, :])
                    last.then_inc(put, 1)
                pe.wait_ge(x1_made, GR)
                for g in range(GR):
                    pe.wait_ge(h_made, g + 1)
                    if g >= 6:
                        pe.wait_ge(took, g - 5)
                    for c in range(4):
                        last = nc.tensor.transpose(banks[g % 6][:, c * P:(c + 1) * P], h[:, g * 4 + c, :], ident32[:, :])
                    last.then_inc(put, 1)
                pe.wait_ge(w_in, 48)
                for g in range(GR):
                    pe.wait_ge(took, max(g + 1, GR + g - 5))
                    nc.tensor.matmul(banks[(GR + g) % 6][:, :], w_sb[:, :], group(h_t, g), start=True, stop=True).then_inc(put, 1)
                for g in range(GR):
                    pe.wait_ge(took, 2 * GR + g - 5)
                    for c in range(4):
                        last = nc.tensor.matmul(banks[(2 * GR + g) % 6][:, c * P:(c + 1) * P], h_t[:, (g * 4 + c) * P:(g * 4 + c + 1) * P], w_sb[:, :],
                                                start=True, stop=True)
                    last.then_inc(put, 1)
                pe.wait_ge(mom_made, 2)
                for g in range(GR):
                    pe.wait_ge(took, max(GR + g + 1, 3 * GR + g - 5))
                    nc.tensor.matmul(banks[(3 * GR + g) % 6][:, :], a2_wide[:, :], group(wh_t, g), start=True, stop=True).then_inc(put, 1)
                for c in range(C):
                    last = nc.tensor.matmul(s_ps[:, c:c + 1], wh_t[:, c * P:(c + 1) * P], a1[:, :], start=True, stop=True)
                last.then_inc(s_put, 1)

            @block.scalar
            def _(act):
                act.wait_ge(mom_made, 1)
                act.wait_ge(eps_made, 1)
                nc.scalar.activation(std[:, :], mom[:, :, 1], ACT.Sqrt, bias=eps[:, :]).then_inc(std_made, 1)
                for i in range(4 * GR):
                    g = i % GR
                    act.wait_ge(put, GR + i + 1)
                    src = banks[i % 6][:, :]
                    if i // GR == 2:
                        dst, src = wh[:, g * 4:(g + 1) * 4, 0:D], src.rearrange("p (c d) -> p c d", d=D)
                    else:
                        dst = group((h_t, wh_t, None, score_t)[i // GR], g)
                    nc.scalar.activation(dst, src, ACT.Copy).then_inc(took, 1)
                act.wait_ge(s_put, 1)
                nc.scalar.activation(score_s[:, :], s_ps[:, :], ACT.Copy)

            @block.vector
            def _(dve):
                n = [0]

                def link(ins):
                    n[0] += 1
                    ins.then_inc(step, 1)
                    dve.wait_ge(step, n[0])

                nc.vector.memset(eps[:, :], EPS).then_inc(eps_made, 1)
                nc.vector.memset(wh[:, :, D:D + 1], 1.0)
                link(nc.vector.memset(ones[:, :], 1.0))
                dve.wait_ge(x_in, 16)
                for g in range(GR):
                    dve.wait_ge(put, g + 1)
                    xg = x1[:, g * 4:(g + 1) * 4, :].rearrange("p c d -> p (c d)")
                    nc.vector.scalar_tensor_tensor(out=xg, in0=banks[g % 6][:, :], scalar=1.0 / HSCALE, in1=xg,
                                                   op0=ALU.mult, op1=ALU.add).then_inc(x1_made, 1)
                dve.wait_ge(x1_made, GR)
                for c in range(C):
                    last = nc.vector.bn_stats(stats[:, c, :], x1[:, c, :])
                link(last)
                for c in range(C):
                    last = nc.vector.bn_aggr(mom[:, c, :], stats[:, c, :])
                last.then_inc(mom_made, 1)
                dve.wait_ge(w_in, 48)
                nc.vector.tensor_scalar(a2_wide[:, :], ones[:, :], a2[:, :], None, ALU.mult).then_inc(mom_made, 1)
                dve.wait_ge(std_made, 1)
                link(nc.vector.reciprocal(rstd[:, :], std[:, :]))
                link(nc.vector.tensor_tensor(std[:, :], rstd[:, :], rstd[:, :], ALU.mult))
                link(nc.vector.scalar_tensor_tensor(out=std[:, :], in0=mom[:, :, 1], scalar=eps[:, :], in1=std[:, :],
                                                    op0=ALU.add, op1=ALU.mult))
                link(nc.vector.tensor_scalar(std[:, :], std[:, :], -0.5, 1.5, ALU.mult, ALU.add))
                link(nc.vector.tensor_tensor(rstd[:, :], rstd[:, :], std[:, :], ALU.mult))
                for g in range(GR):
                    for c in range(g * 4, g * 4 + 4):
                        last = nc.vector.tensor_scalar(h[:, c, :], x1[:, c, :], mom[:, c, 0:1], rstd[:, c:c + 1], ALU.subtract, ALU.mult)
                    link(last)
                    hg = h[:, g * 4:(g + 1) * 4, :]
                    nc.vector.tensor_scalar(hg, hg, 0.0, None, ALU.max).then_inc(h_made, 1)


def attend(nc, absent_rows, out_rows, ident32, x1, wh, score_t, score_s):
    ctx = ExitStack()
    with ctx:
        sb = lambda name, shape, dt: ctx.enter_context(nc.sbuf_tensor(name, shape, dt))
        sem = lambda name: ctx.enter_context(nc.semaphore(name))
        RING = 4
        GR = C // 4
        PARTS = 4
        PW = N // PARTS
        OUTER = N // P // RING
        y = sb("y", [P, RING, N], F32)
        gone = sb("gone", [P, 2, N], BF16)
        turned = sb("turned", [P, 4, 512], F32)
        z = sb("z", [P, 2, N], F32)
        top = sb("top", [P, RING, PARTS], F32)
        row = sb("row", [P, RING, 8], F32)
        rden = sb("rden", [P, RING], F32)
        att = sb("att", [P, 2, RING, D], F32)
        low = sb("low", [P, 2, RING, D], F32)
        turn_ps = [ctx.enter_context(nc.psum_tensor(f"turn_ps{i}", [P, 512], F32)) for i in range(4)]
        out_ps = [ctx.enter_context(nc.psum_tensor(f"out_ps{i}", [P, D + 1], F32)) for i in range(2)]
        gone_in = [sem(f"gone_in{i}") for i in range(2)]
        scored = sem("scored")
        row_step = sem("row_step")
        biased = sem("biased")
        weighed = sem("weighed")
        blended = sem("blended")
        turned_g = sem("turned_g")
        moved_a, moved_v = sem("moved_a"), sem("moved_v")
        mixed = sem("mixed")
        rden_made = sem("rden_made")
        normed = sem("normed")
        low_made, low_exp, fin_step = sem("low_made"), sem("low_exp"), sem("fin_step")
        att_free, low_free, finished = sem("att_free"), sem("low_free"), sem("finished")
        stored = sem("stored")
        passed_p, passed_a, passed_v, passed_sp = (sem("passed_" + e) for e in "pavs")
        BY_ACT = (0, 1, 2, 4, 5, 6)
        BY_DVE = (3, 7)
        NA, NV = len(BY_ACT), len(BY_DVE)

        def all_tiles(eng, tiles):
            tiles(0, 0, True, False)
            with eng.Fori(0, OUTER // 2 - 1) as oo:
                tiles(oo * 2 + 1, 1, False, False)
                tiles(oo * 2 + 2, 0, False, False)
            tiles(OUTER - 1, 1, False, True)

        with nc.Block() as block:
            @block.sync
            def _(sp):
                def load(r, slot):
                    sp.dma_start(gone[:, slot, :], absent_rows[bass.ds(r * P, P), :]).then_inc(gone_in[slot], 16)

                def store(o, k):
                    wait_apart(sp, finished, o + 1, passed_sp)
                    sp.dma_start(out_rows[:, bass.ds(o * RING, RING), :], low[:, k, :, :]).then_inc(stored, 16)
                    wait_apart(sp, stored, (o + 1) * 16, passed_sp)
                    sp.sem_inc(low_free, 1)

                def tiles(o, k, first, last):
                    for b in range(RING):
                        if not (last and b >= RING - 2):
                            wait_apart(sp, scored, (o * RING + b + 1) * PARTS, passed_sp)
                            load(o * RING + b + 2, b % 2)
                        if b == 2 and not first:
                            store(o - 1, 1 - k)

                sp.sem_inc(low_free, 2)
                load(0, 0)
                load(1, 1)
                all_tiles(sp, tiles)
                store(OUTER - 1, 1)

            @block.vector
            def _(dve):
                def score(o, b, part):
                    if part == 0:
                        wait_apart(dve, gone_in[b % 2], 16 * (o * (RING // 2) + b // 2 + 1), passed_v)
                    nc.vector.tensor_tensor_reduce(out=y[:, b % RING, part * PW:(part + 1) * PW],
                                                   in0=score_t[:, part * PW:(part + 1) * PW],
                                                   in1=gone[:, b % 2, part * PW:(part + 1) * PW],
                                                   scale=1.0, scalar=-3e38, op0=ALU.subtract, op1=ALU.max,
                                                   accum_out=top[:, b % RING, part:part + 1]).then_inc(scored, 1)

                def blend(o, b, part):
                    yy = y[:, b % RING, part * PW:(part + 1) * PW]
                    dve.wait_ge(weighed, PARTS * (o * RING + b) + part + 1)
                    nc.vector.tensor_tensor(yy, yy, z[:, b % 2, part * PW:(part + 1) * PW], ALU.max).then_inc(blended, 1)

                def move(r, i):
                    g = BY_DVE[i]
                    dve.wait_ge(turned_g, (r + 2) * GR + g + 1)
                    dve.wait_ge(mixed, r * GR + g + 1)
                    nc.vector.tensor_copy(turned[:, g % 4, :], turn_ps[g % 4][:, :]).then_inc(moved_v, 1)

                def norm(o, b, k):
                    r = o * RING + b
                    if b == 0:
                        dve.wait_ge(att_free, o + 1)
                    dve.wait_ge(mixed, (r + 1) * GR + 4)
                    nc.vector.reciprocal(rden[:, b:b + 1], out_ps[b % 2][:, D:D + 1]).then_inc(rden_made, 1)
                    dve.wait_ge(rden_made, r + 1)
                    nc.vector.tensor_scalar(att[:, k, b, :], out_ps[b % 2][:, 0:D], rden[:, b:b + 1], None, ALU.mult).then_inc(normed, 1)

                def tiles(o, k, first, last):
                    for b in range(RING):
                        r = o * RING + b
                        for what, i in (("blend", 0), ("score", 0), ("blend", 1), ("move", 0), ("norm", 0), ("score", 1), ("blend", 2),
                                        ("score", 2), ("blend", 3), ("move", 1), ("score", 3)):
                            if what == "blend" and not (last and b == RING - 1):
                                blend(o, b + 1, i)
                            elif what == "score" and not (last and b >= RING - 3):
                                if i == 0:
                                    dve.wait_ge(turned_g, (r + 2) * GR)
                                score(o, b + 3, i)
                            elif what == "move":
                                move(r, i)
                            elif what == "norm" and not (first and b == 0):
                                norm(o if b else o - 1, b - 1 if b else RING - 1, k if b else 1 - k)

                dve.sem_inc(att_free, 2)
                dve.sem_inc(moved_v, NV)
                dve.sem_inc(normed, 2)
                for b in range(3):
                    for part in range(PARTS):
                        score(0, b, part)
                for part in range(PARTS):
                    blend(0, 0, part)
                all_tiles(dve, tiles)
                norm(OUTER - 1, RING - 1, 1)

            @block.scalar
            def _(act):
                def weigh(o, b, part, second):
                    r, yy, zz = o * RING + b, y[:, b % RING, part * PW:(part + 1) * PW], z[:, b % 2, part * PW:(part + 1) * PW]
                    if not second:
                        act.wait_ge(biased, 2 * r + 2)
                        act.wait_ge(blended, PARTS * r + part + 1)
                        nc.scalar.activation(zz, yy, ACT.Exp, scale=ALPHA, bias=row[:, b % RING, 4:5])
                    else:
                        nc.scalar.activation(yy, yy, ACT.Exp, bias=row[:, b % RING, 3:4]).then_inc(weighed, 1)

                def move(r, i):
                    g = BY_ACT[i]
                    act.wait_ge(turned_g, (r + 2) * GR + g + 1)
                    act.wait_ge(mixed, r * GR + g + 1)
                    nc.scalar.activation(turned[:, g % 4, :], turn_ps[g % 4][:, :], ACT.Copy).then_inc(moved_a, 1)

                def exp_low(o, k):
                    act.wait_ge(low_made, o + 1)
                    nc.scalar.activation(low[:, k, :, :], low[:, k, :, :], ACT.Exp).then_inc(low_exp, 1)

                def tiles(o, k, first, last):
                    for b in range(RING):
                        r = o * RING + b
                        ahead = not (last and b >= RING - 2)
                        for it in ((0, 0), 0, (0, 1), 1, (1, 0), 2, (1, 1), (2, 0), 3, (2, 1), 4, (3, 0), 5, (3, 1)):
                            if isinstance(it, int):
                                move(r, it)
                            elif ahead:
                                weigh(o, b + 2, *it)
                        if b == 0 and not first:
                            exp_low(o - 1, 1 - k)

                act.sem_inc(blended, 2 * PARTS)
                act.sem_inc(moved_a, NA)
                for b in range(2):
                    for part in range(PARTS):
                        weigh(0, b, part, 0)
                        weigh(0, b, part, 1)
                all_tiles(act, tiles)
                exp_low(OUTER - 1, 1)

            @block.tensor
            def _(pe):
                def wait_moved(r, g):
                    if g in BY_ACT:
                        pe.wait_ge(moved_a, (r + 1) * NA + BY_ACT.index(g) + 1)
                    else:
                        pe.wait_ge(moved_v, (r + 1) * NV + BY_DVE.index(g) + 1)

                def turn(r, b, g):
                    r, b, g = r + g // GR, b + g // GR, g % GR
                    pe.wait_ge(blended, PARTS * (r + 2) + g // (GR // PARTS) + 1)
                    wait_moved(r if g >= 4 else r - 1, (g - 4) % GR)
                    for c in range(4):
                        last = nc.tensor.transpose(turn_ps[g % 4][:, c * P:(c + 1) * P], y[:, b % RING, (g * 4 + c) * P:(g * 4 + c + 1) * P],
                                                   ident32[:, :])
                    last.then_inc(turned_g, 1)

                def mix(r, b, g):
                    wait_moved(r, g)
                    if g == 0:
                        pe.wait_ge(normed, r + 1)
                    for c in range(4):
                        last = nc.tensor.matmul(out_ps[b % 2][:, :], turned[:, g % 4, c * P:(c + 1) * P], wh[:, g * 4 + c, :],
                                                start=g == 0 and c == 0, stop=g == GR - 1 and c == 3)
                    last.then_inc(mixed, 1)

                def tiles(o, k, first, last):
                    for b in range(RING):
                        for g in range(GR):
                            if not (last and b == RING - 1 and g + 3 >= GR):
                                turn(o * RING + b, b, g + 3)
                            mix(o * RING + b, b, g)

                pe.sem_inc(turned_g, 2 * GR)
                pe.sem_inc(mixed, 4)
                for g in range(3):
                    turn(0, 0, g)
                all_tiles(pe, tiles)

            @block.gpsimd
            def _(pool):
                def cut(o, k):
                    pool.wait_ge(low_free, o + 1)
                    wait_apart(pool, normed, (o + 1) * RING + 2, passed_p)
                    nc.gpsimd.tensor_scalar(low[:, k, :, :], att[:, k, :, :], 0.0, None, ALU.min).then_inc(low_made, 1)
                    nc.gpsimd.tensor_scalar(att[:, k, :, :], att[:, k, :, :], 0.0, -1.0, ALU.max, ALU.add).then_inc(fin_step, 1)
                    wait_apart(pool, fin_step, 2 * o + 1, passed_p)
                    nc.gpsimd.tensor_tensor(att[:, k, :, :], att[:, k, :, :], x1[:, bass.ds(o * RING, RING), :], ALU.add).then_inc(fin_step, 1)

                def finish(o, k):
                    wait_apart(pool, fin_step, 2 * o + 2, passed_p)
                    wait_apart(pool, low_exp, o + 1, passed_p)
                    nc.gpsimd.tensor_tensor(low[:, k, :, :], low[:, k, :, :], att[:, k, :, :], ALU.add).then_inc(finished, 1)
                    pool.wait_ge(finished, o + 1)
                    pool.sem_inc(att_free, 1)

                def bias(o, b):
                    r, at = o * RING + b, b % RING
                    col = lambda i: row[:, at, i:i + 1]
                    n = [0]

                    def step(ins):
                        n[0] += 1
                        ins.then_inc(row_step, 1)
                        wait_apart(pool, row_step, r * 4 + n[0], passed_p)

                    step(nc.gpsimd.tensor_copy(col(0), score_s[:, bass.ds(r, 1)]))
                    wait_apart(pool, scored, PARTS * (r + 1), passed_p)
                    step(nc.gpsimd.tensor_scalar(col(5), top[:, at, 0:1], top[:, at, 1:2], top[:, at, 2:3], ALU.max, ALU.max))
                    step(nc.gpsimd.tensor_scalar(col(1), col(5), top[:, at, 3:4], col(0), ALU.max, ALU.add))
                    step(nc.gpsimd.tensor_scalar(col(2), col(1), ALPHA, col(1), ALU.mult, ALU.max))
                    nc.gpsimd.tensor_scalar(col(3), col(0), col(2), None, ALU.subtract).then_inc(biased, 1)
                    nc.gpsimd.tensor_scalar(col(4), col(0), ALPHA, col(2), ALU.mult, ALU.subtract).then_inc(biased, 1)

                def tiles(o, k, first, last):
                    for b in range(RING):
                        bias(o, b)
                        if b == 2 and not first:
                            cut(o - 1, 1 - k)
                        if b == 3 and not first:
                            finish(o - 1, 1 - k)

                all_tiles(pool, tiles)
                cut(OUTER - 1, 1)
                finish(OUTER - 1, 1)


def kernel(x, adj, L1_gnn_W, L1_gnn_a):
    import numpy as np
    import concourse.bacc as bacc
    from concourse.bass_utils import run_bass_kernel_spmd as run
    nc = bacc.Bacc("TRN2", target_bir_lowering=False, num_devices=1)
    arrays, args = {}, []
    for name, arr in (("x", x), ("adj", adj), ("w", L1_gnn_W), ("a", L1_gnn_a)):
        arr = np.ascontiguousarray(arr)
        arrays[name] = arr
        args.append(nc.dram_tensor(name, arr.shape, mybir.dt.from_np(arr.dtype), kind="ExternalInput").ap())
    out = nc.dram_tensor("out", (N, D), F32, kind="ExternalOutput").ap()
    gnn_two_layers(nc, *args, out)
    result = run(nc, [arrays], core_ids=[0])
    return result.results[0]["out"]
```

```python
import concourse.bass as bass
from concourse import mybir
from contextlib import ExitStack

F32, F16, BF16, I32 = mybir.dt.float32, mybir.dt.float16, mybir.dt.bfloat16, mybir.dt.int32
ALU, ACT, AX = mybir.AluOpType, mybir.ActivationFunctionType, mybir.AxisListType

P = 128
N = 4096
D = 128
C = N // P
TI = 512
TILES = N // TI
ROWS = TI // P
PAIR = 2
STEPS = C // PAIR
UNIT = 4
UNITS = STEPS // UNIT
UCOLS = UNIT * PAIR * P
W = PAIR * TI
ROUNDS = 4
MARK = 1024.0
HSCALE = 4096.0
EPS = 1e-5
FAR = 2.0 ** 93
ALPHA = 0.2


def gnn_two_layers(nc, x, adj, w, a, out):
    ctx = ExitStack()
    with ctx:
        def sb(name, shape, dt, at=None):
            return (at or ctx).enter_context(nc.sbuf_tensor(name, shape, dt))

        ident_b = sb("ident_b", [P, P], BF16)
        ident32 = sb("ident32", [P, P], F32)
        order_w = sb("order_w", [P, P], F16)
        diff_i = sb("diff_i", [P, P], I32)
        diff = sb("diff", [P, P], F32)
        rank_i = sb("rank_i", [P, P], I32)
        rank_tab = sb("rank_tab", [P, P], F32)
        chunk_i = sb("chunk_i", [C, 1], I32)
        chunk_no = sb("chunk_no", [C, 1], F32)
        best = sb("best", [P, N], F32)

        x_rows = x.rearrange("(c p) d -> p c d", p=P)
        out_rows = out.rearrange("(c p) d -> p c d", p=P)

        absent_rows = nc.dram_tensor("absent_rows", (N, N), BF16).ap()

        with ExitStack() as layer0:
            h_hi = sb("h_hi", [P, C, D], F16, layer0)
            h_lo = sb("h_lo", [P, C, D], F16, layer0)
            prepare(nc, x_rows, h_hi, h_lo, ident_b, ident32, order_w, diff_i, diff, rank_i, rank_tab, chunk_i, chunk_no)
            neighbour_max(nc, adj, absent_rows, h_hi, h_lo, ident_b, order_w, rank_tab, chunk_no, best)
        with ExitStack() as layer1:
            x1 = sb("x1", [P, C, D], F32, layer1)
            wh = sb("wh", [P, C, D + 1], F32, layer1)
            score_t = sb("score_t", [P, N], F32, layer1)
            score_s = sb("score_s", [P, C], F32, layer1)
            project(nc, x_rows, w, a, ident32, best, x1, wh, score_t, score_s)
            attend(nc, absent_rows, out_rows, ident32, x1, wh, score_t, score_s)


def wait_apart(eng, sem, value, passed):
    eng.wait_ge(sem, value)
    eng.sem_inc(passed, 1)


def prepare(nc, x_rows, h_hi, h_lo, ident_b, ident32, order_w, diff_i, diff, rank_i, rank_tab, chunk_i, chunk_no):
    ctx = ExitStack()
    with ctx:
        xs = ctx.enter_context(nc.sbuf_tensor("xs", [P, C, D], F32))
        hs = ctx.enter_context(nc.sbuf_tensor("hs", [P, C, D], F32))
        stats = ctx.enter_context(nc.sbuf_tensor("ln1_stats", [P, C, 6], F32))
        mom = ctx.enter_context(nc.sbuf_tensor("ln1_mom", [P, C, 2], F32))
        std = ctx.enter_context(nc.sbuf_tensor("ln1_std", [P, C], F32))
        rstd = ctx.enter_context(nc.sbuf_tensor("ln1_rstd", [P, C], F32))
        eps = ctx.enter_context(nc.sbuf_tensor("ln1_eps", [P, 1], F32))
        sem = lambda name: ctx.enter_context(nc.semaphore(name))
        x_in = [sem(f"x_in{i}") for i in range(4)]
        iotas, consts, var_ready, std_ready, step = sem("iotas"), sem("consts"), sem("var_ready"), sem("std_ready"), sem("ln1_step")
        hs_ready, hi_ready = sem("hs_ready"), sem("hi_ready")
        G = C // 4
        with nc.Block() as block:
            @block.sync
            def _(sp):
                for i in range(4):
                    sp.dma_start(xs[:, i * G:(i + 1) * G, :], x_rows[:, i * G:(i + 1) * G, :]).then_inc(x_in[i], 16)

            @block.gpsimd
            def _(pool):
                pool.iota(diff_i[:, :], pattern=[[1, P]], base=0, channel_multiplier=-1).then_inc(iotas, 1)
                pool.iota(rank_i[:, :], pattern=[[1, P]], base=-int(MARK), channel_multiplier=0).then_inc(iotas, 1)
                pool.iota(chunk_i[:, :], pattern=[[1, 1]], base=0, channel_multiplier=1).then_inc(iotas, 1)

            @block.scalar
            def _(act):
                act.wait_ge(var_ready, 1)
                nc.scalar.activation(std[:, :], mom[:, :, 1], ACT.Sqrt, bias=eps[:, :]).then_inc(std_ready, 1)
                act.wait_ge(hs_ready, 1)
                nc.scalar.activation(h_hi[:, :, :], hs[:, :, :], ACT.Copy).then_inc(hi_ready, 1)

            @block.vector
            def _(dve):
                n = [0]

                def link(ins):
                    n[0] += 1
                    ins.then_inc(step, 1)
                    dve.wait_ge(step, n[0])

                nc.vector.memset(eps[:, :], EPS)
                dve.wait_ge(iotas, 3)
                nc.vector.tensor_copy(rank_tab[:, :], rank_i[:, :])
                nc.vector.tensor_copy(chunk_no[:, :], chunk_i[:, :])
                link(nc.vector.tensor_copy(diff[:, :], diff_i[:, :]))
                nc.vector.tensor_scalar(ident_b[:, :], diff[:, :], 0.0, None, ALU.is_equal)
                link(nc.vector.tensor_scalar(ident32[:, :], diff[:, :], 0.0, -MARK, ALU.is_equal, ALU.mult))
                link(nc.vector.scalar_tensor_tensor(out=order_w[:, :], in0=diff[:, :], scalar=0.0, in1=ident32[:, :],
                                                    op0=ALU.is_gt, op1=ALU.add))
                nc.vector.tensor_scalar(ident32[:, :], diff[:, :], 0.0, None, ALU.is_equal)
                for i in range(4):
                    dve.wait_ge(x_in[i], 16)
                    for c in range(i * G, (i + 1) * G):
                        last = nc.vector.bn_stats(stats[:, c, :], xs[:, c, :])
                link(last)
                for c in range(C):
                    last = nc.vector.bn_aggr(mom[:, c, :], stats[:, c, :])
                last.then_inc(var_ready, 1)
                dve.wait_ge(std_ready, 1)
                link(nc.vector.reciprocal(rstd[:, :], std[:, :]))
                link(nc.vector.tensor_tensor(std[:, :], rstd[:, :], rstd[:, :], ALU.mult))
                link(nc.vector.scalar_tensor_tensor(out=std[:, :], in0=mom[:, :, 1], scalar=eps[:, :], in1=std[:, :],
                                                    op0=ALU.add, op1=ALU.mult))
                link(nc.vector.tensor_scalar(std[:, :], std[:, :], -0.5, 1.5, ALU.mult, ALU.add))
                link(nc.vector.tensor_tensor(rstd[:, :], rstd[:, :], std[:, :], ALU.mult))
                for c in range(C):
                    last = nc.vector.tensor_scalar(hs[:, c, :], xs[:, c, :], mom[:, c, 0:1], rstd[:, c:c + 1],
                                                   ALU.subtract, ALU.mult)
                link(last)
                link(nc.vector.tensor_scalar(hs[:, :, :], hs[:, :, :], 0.0, HSCALE, ALU.max, ALU.mult))
                nc.vector.sem_inc(hs_ready, 1)
                dve.wait_ge(hi_ready, 1)
                nc.vector.tensor_tensor(h_lo[:, :, :], hs[:, :, :], h_hi[:, :, :], ALU.subtract)


def neighbour_max(nc, adj, absent_rows, h_hi, h_lo, ident_b, order_w, rank_tab, chunk_no, best):
    ctx = ExitStack()
    with ctx:
        sb = lambda name, shape, dt: ctx.enter_context(nc.sbuf_tensor(name, shape, dt))
        ps = lambda name, shape, dt: ctx.enter_context(nc.psum_tensor(name, shape, dt))
        sem = lambda name: ctx.enter_context(nc.semaphore(name))
        stage = sb("stage", [P, 2, ROWS, UCOLS], I32)
        absent = sb("absent", [P, 2, ROWS, UCOLS], BF16)
        edge_t = sb("edge_t", [P, W], F16)
        order = sb("order", [P, 2, C, TI], F16)
        sel0, sel1 = sb("sel0", [P, 2, W], F16), sb("sel1", [P, 2, W], F16)
        sel2, sel3 = sb("sel2", [P, W], F16), sb("sel3", [P, W], F16)
        acc = sb("acc", [P, 2, 2, W], F32)
        xsel = sb("xsel", [P, TI], F16)
        neg = sb("neg", [P, 1], F32)
        far = sb("far", [P, 1], F32)
        last_row = sb("last_row", [C, TI], F16)
        lr_flag = sb("lr_flag", [C, TI], F32)
        lr_cnt = sb("lr_cnt", [C, TI], F32)
        key_sq = sb("key_sq", [32, 32], F32)
        key_row = sb("key_row", [32, 32], F32)
        key_sorted = sb("key_sorted", [1, C], F32)
        key_int = sb("key_int", [1, C], I32)
        x_entry = sb("x_entry", [1, C], I32)
        x_shift = sb("x_shift", [1, C], I32)
        x_deg = sb("x_deg", [1, C], I32)
        x_degf = sb("x_degf", [1, C], F32)
        x_extra = sb("x_extra", [1, C + 1], F32)
        x_scan = sb("x_scan", [1, C + 1], F32)
        zeros = sb("zeros", [1, C + 1], F32)
        x_has = sb("x_has", [1, C], F32)
        x_count = sb("x_count", [1, 1], F32)
        x_counti = sb("x_counti", [1, 1], I32)
        x_start = sb("x_start", [1, C + 1], I32)

        flip_ps = ps("flip_ps", [P, W], BF16)
        order_ps = ps("order_ps", [P, W], F32)
        pick_ps = [ps(f"pick_ps{i}", [P, W], F32) for i in range(2)]
        extra_ps = ps("extra_ps", [P, TI], F32)

        landed = [sem(f"landed{i}") for i in range(2)]
        kept = [sem(f"kept{i}") for i in range(2)]
        absent_free = sem("absent_free")
        mask_ready = sem("mask_ready")
        flipped = sem("flipped")
        edge_ready = sem("edge_ready")
        ordered = sem("ordered")
        sel0_ready = sem("sel0_ready")
        order_ready = sem("order_ready")
        sel1_ready = sem("sel1_ready")
        sel_ready = sem("sel_ready")
        picked = sem("picked")
        pick_free = sem("pick_free")
        row_in = sem("row_in")
        row_free = sem("row_free")
        plan_ready = sem("plan_ready")
        plan_read = sem("plan_read")
        extras_done = sem("extras_done")
        xsel_ready = sem("xsel_ready")
        xpicked = sem("xpicked")
        xkept = sem("xkept")
        step = sem("l0_step")
        passed_pool, passed_pe, passed_dve, passed_sp = (sem("passed_" + e) for e in ("pool", "pe", "dve", "sp"))
        neg_ready = sem("neg_ready")
        folded = sem("folded")
        acc_clear = sem("acc_clear")

        def order_of(b, p):
            return order[:, b, p * PAIR:(p + 1) * PAIR, :].rearrange("p c i -> p (c i)")

        def load_unit(sp, q, u, slot):
            sp.dma_start(stage[:, slot, :, :],
                         adj[bass.ds(q * TI, TI), u * UCOLS:(u + 1) * UCOLS].rearrange("(r p) j -> p r j", p=P)
                         ).then_inc(landed[slot], 16)

        def keep_unit(sp, q, u):
            sp.dma_start(absent_rows[bass.ds(q * TI, TI), u * UCOLS:(u + 1) * UCOLS].rearrange("(r p) j -> p r j", p=P),
                         absent[:, u % 2, :, :]).then_inc(kept[u % 2], 16)

        with nc.Block() as block:
            @block.sync
            def _(sp):
                sp.sem_inc(absent_free, 2)
                load_unit(sp, 0, 0, 0)
                load_unit(sp, 0, 1, 1)

                def tile(q, b, last):
                    for u in range(UNITS):
                        wait_apart(sp, mask_ready, (q * UNITS + u + 1) * UNIT, passed_sp)
                        keep_unit(sp, q, u)
                        if not (last and u + 2 >= UNITS):
                            load_unit(sp, q + (u + 2) // UNITS, (u + 2) % UNITS, u % 2)
                        wait_apart(sp, kept[u % 2], 16 * (q * (UNITS // 2) + u // 2 + 1), passed_sp)
                        sp.sem_inc(absent_free, 1)
                    wait_apart(sp, order_ready, q * STEPS + STEPS, passed_sp)
                    wait_apart(sp, row_free, q + 1, passed_sp)
                    sp.dma_start(last_row[:, :], order[P - 1:P, b, :, :]).then_inc(row_in, 16)

                with sp.Fori(0, TILES // 2 - 1) as qq:
                    for b in range(2):
                        tile(qq * 2 + b, b, False)
                for b in range(2):
                    tile(TILES - 2 + b, b, b == 1)
            @block.gpsimd
            def _(pool):
                def tile(q, b):
                    for p in range(STEPS):
                        if p == STEPS // 2 + 2:
                            wait_apart(pool, folded, q + 1, passed_pool)
                            nc.gpsimd.memset(acc[:, 1 - b, :, :], 0.0).then_inc(acc_clear, 1)
                        wait_apart(pool, order_ready, q * STEPS + p + 1, passed_pool)
                        nc.gpsimd.tensor_scalar(sel1[:, p % 2, :], order_of(b, p), 1 - MARK, None, ALU.is_equal).then_inc(sel1_ready, 1)

                with pool.Fori(0, TILES // 2) as qq:
                    for b in range(2):
                        tile(qq * 2 + b, b)

            @block.scalar
            def _(act):
                def convert(u, s):
                    nc.scalar.activation(absent[:, u % 2, :, s * PAIR * P:(s + 1) * PAIR * P],
                                         stage[:, u % 2, :, s * PAIR * P:(s + 1) * PAIR * P],
                                         ACT.Relu, scale=-FAR, bias=far[:, :]).then_inc(mask_ready, 1)

                def edges(g):
                    act.wait_ge(flipped, g + 1)
                    nc.scalar.activation(edge_t[:, :], flip_ps[:, :], ACT.Relu, scale=-1.0, bias=1.0).then_inc(edge_ready, 1)

                def keep_order(g, b, p):
                    act.wait_ge(ordered, g + 1)
                    nc.scalar.activation(sel0[:, p % 2, :], order_ps[:, :], ACT.Relu, scale=-1.0, bias=neg[:, :]).then_inc(sel0_ready, 1)
                    nc.scalar.activation(order_of(b, p), order_ps[:, :], ACT.Copy).then_inc(order_ready, 1)

                def tile(q, b, last):
                    for p in range(STEPS):
                        g, u, s = q * STEPS + p, p // UNIT, p % UNIT
                        if p == STEPS - 1 and not last:
                            act.wait_ge(extras_done, q + 1)
                        if not (last and p == STEPS - 1):
                            keep_order(g + 1, (b + (p + 1) // STEPS) % 2, (p + 1) % STEPS)
                        if not (last and p >= STEPS - 2):
                            edges(g + 2)
                        if not (last and u == UNITS - 1):
                            if s == 0:
                                act.wait_ge(landed[(u + 1) % 2], 16 * (2 * q + (u + 1) // 2 + 1))
                                act.wait_ge(absent_free, q * UNITS + u + 2)
                            convert(u + 1, s)

                act.wait_ge(neg_ready, 2)
                act.wait_ge(landed[0], 16)
                for s in range(UNIT):
                    convert(0, s)
                edges(0)
                keep_order(0, 0, 0)
                edges(1)
                with act.Fori(0, TILES // 2 - 1) as qq:
                    for b in range(2):
                        tile(qq * 2 + b, b, False)
                for b in range(2):
                    tile(TILES - 2 + b, b, b == 1)

            @block.tensor
            def _(pe):
                def flip(g, p):
                    u, s = p // UNIT, p % UNIT
                    pe.wait_ge(mask_ready, g + 1)
                    for c in range(PAIR):
                        for r in range(ROWS):
                            last = nc.tensor.transpose(flip_ps[:, c * TI + r * P:c * TI + (r + 1) * P],
                                                       absent[:, u % 2, r, (s * PAIR + c) * P:(s * PAIR + c + 1) * P],
                                                       ident_b[:, :])
                    last.then_inc(flipped, 1)

                def rank(g):
                    pe.wait_ge(edge_ready, g + 1)
                    pe.wait_ge(order_ready, g)
                    for c in range(PAIR):
                        last = nc.tensor.matmul(order_ps[:, c * TI:(c + 1) * TI], order_w[:, :], edge_t[:, c * TI:(c + 1) * TI],
                                                start=True, stop=True)
                    last.then_inc(ordered, 1)

                def pick(g, p, k):
                    if k == 0:
                        pe.wait_ge(sel0_ready, g + 1)
                    elif k == 1:
                        pe.wait_ge(sel1_ready, g + 1)
                    else:
                        pe.wait_ge(sel_ready, g * (ROUNDS - 2) + k - 1)
                    pe.wait_ge(pick_free, g * ROUNDS + k + 1)
                    s = (sel0[:, p % 2, :], sel1[:, p % 2, :], sel2, sel3)[k]
                    dst = pick_ps[k % 2]
                    for c in range(PAIR):
                        for part, h in enumerate((h_hi, h_lo)):
                            last = nc.tensor.matmul(dst[:, c * TI:(c + 1) * TI], h[:, p * PAIR + c, :], s[:, c * TI:(c + 1) * TI],
                                                    start=part == 0, stop=part == 1)
                    last.then_inc(picked, 1)

                def extras(q):
                    wait_apart(pe, plan_ready, q + 1, passed_pe)
                    count = pe.value_load(x_counti[0:1, 0:1], min_val=0, max_val=C)
                    with pe.If(count > 0):
                        with pe.Fori(0, count) as e:
                            entry = pe.value_load(x_entry[0:1, bass.ds(e, 1)], min_val=0, max_val=2 ** 30)
                            c = pe.snap(entry & (C - 1), min_val=0, max_val=C - 1)
                            deg = pe.snap((entry >> 5) & 255).with_bounds(min_val=ROUNDS + 1, max_val=P)
                            start = pe.snap(entry >> 13, min_val=0, max_val=C * TILES * P)
                            with pe.Fori(ROUNDS, deg) as k:
                                pe.wait_ge(xsel_ready, start + k - ROUNDS + 1)
                                for part, h in enumerate((h_hi, h_lo)):
                                    last = nc.tensor.matmul(extra_ps[:, :], h[:, bass.ds(c, 1), :].rearrange("p c d -> p (c d)"),
                                                            xsel[:, :], start=part == 0, stop=part == 1)
                                last.then_inc(xpicked, 1)
                    pe.end_ifs()
                    pe.sem_inc(plan_read, 1)

                def tile(q, last):
                    for p in range(STEPS):
                        g = q * STEPS + p
                        if not (last and p == STEPS - 1):
                            rank(g + 1)
                        if not (last and p >= STEPS - 2):
                            flip(g + 2, (p + 2) % STEPS)
                        for k in range(ROUNDS):
                            pick(g, p, k)
                        if p == STEPS // 2 - 1:
                            extras(q)

                pe.sem_inc(plan_read, 1)
                flip(0, 0)
                rank(0)
                flip(1, 1)
                with pe.Fori(0, TILES - 1) as q:
                    tile(q, False)
                tile(TILES - 1, True)
                extras(TILES)

            @block.vector
            def _(dve):
                n = [0]

                def link(ins, at=None):
                    n[0] += 1
                    ins.then_inc(step, 1)
                    wait_apart(dve, step, n[0] if at is None else at + n[0], passed_dve)

                nc.vector.memset(far[:, :], FAR).then_inc(neg_ready, 1)
                nc.vector.memset(neg[:, :], 1.0 - MARK).then_inc(neg_ready, 1)
                nc.vector.memset(last_row[:, :], 0.0)
                nc.vector.memset(x_scan[:, :], 0.0)
                nc.vector.memset(key_sq[:, :], 0.0)
                nc.vector.memset(zeros[:, :], 0.0)
                nc.vector.memset(x_extra[:, :], 0.0)
                nc.vector.memset(acc[:, :, :, :], 0.0)
                link(nc.vector.memset(best[:, :], 0.0))
                nc.vector.sem_inc(pick_free, 2)
                nc.vector.sem_inc(row_free, 1)
                nc.vector.sem_inc(xkept, 1)
                pre = n[0]

                def step_maxima(q, b, p, between):
                    dve.wait_ge(order_ready, q * STEPS + p + 1)
                    for k in range(2, ROUNDS):
                        nc.vector.tensor_scalar((sel2, sel3)[k - 2][:, :], order[:, b, bass.ds(p * PAIR, PAIR), :].rearrange("p c i -> p (c i)"),
                                                k - MARK, None, ALU.is_equal).then_inc(sel_ready, 1)
                    for k in range(ROUNDS):
                        between(k)
                        dve.wait_ge(picked, (q * STEPS + p) * ROUNDS + k + 1)
                        dve.wait_ge(pick_free, (q * STEPS + p) * ROUNDS + k + 1)
                        nc.vector.tensor_tensor(acc[:, b, k % 2, :], pick_ps[k % 2][:, :], acc[:, b, k % 2, :],
                                                ALU.max).then_inc(pick_free, 1)

                def maxima(q, b, lo, hi):
                    with dve.Fori(lo, hi) as p:
                        step_maxima(q, b, p, lambda k: None)

                PLAN = 18
                PLAN_STEPS = -(-(PLAN + 1) // ROUNDS)

                def plan(q, i):
                    if i > PLAN:
                        return
                    wait_apart(dve, step, q * (PLAN + 1) + pre + i, passed_dve)
                    V = nc.vector
                    t = (i - 5) // 2 if 5 <= i < 12 else 0
                    top8 = key_sorted[:, t * 8:(t + 1) * 8]
                    if i == 0:
                        if not isinstance(q, int) or q > 0:
                            dve.wait_ge(row_in, q * 16)
                        dve.wait_ge(plan_read, q + 1)
                        ins = V.tensor_scalar(lr_flag[:, :], last_row[:, :], 0.0, MARK + 1.0, ALU.is_lt, ALU.mult)
                    elif i == 1:
                        ins = V.tensor_tensor(lr_cnt[:, :], last_row[:, :], lr_flag[:, :], ALU.add)
                    elif i == 2:
                        ins = V.tensor_reduce(lr_flag[:, 0:1], lr_cnt[:, :], AX.X, ALU.max)
                    elif i == 3:
                        V.sem_inc(row_free, 1)
                        ins = V.scalar_tensor_tensor(out=key_sq[:, 0:1], in0=lr_flag[:, 0:1], scalar=float(C), in1=chunk_no[:, :],
                                                     op0=ALU.mult, op1=ALU.add)
                    elif i == 4:
                        ins = V.transpose(key_row[:, :], key_sq[:, :])
                    elif i < 12 and i % 2 == 1:
                        ins = V.max(top8, key_row[0:1, :])
                    elif i < 12:
                        ins = V.match_replace(out=key_row[0:1, :], in_to_replace=top8, in_values=key_row[0:1, :], imm_value=-1.0)
                    elif i == 12:
                        ins = V.tensor_copy(key_int[:, :], key_sorted[:, :])
                    elif i == 13:
                        ins = V.tensor_scalar(x_deg[:, :], key_int[:, :], 5, None, ALU.logical_shift_right)
                    elif i == 14:
                        V.tensor_scalar(x_has[:, :], x_deg[:, :], ROUNDS + 0.5, 0.0, ALU.is_gt, ALU.add, accum_out=x_count[:, :])
                        V.tensor_scalar(x_extra[:, 1:C + 1], x_deg[:, :], float(ROUNDS), 0.0, ALU.subtract, ALU.max)
                        ins = V.tensor_copy(x_extra[:, 0:1], x_scan[:, C:C + 1])
                    elif i == 15:
                        V.tensor_copy(x_counti[:, :], x_count[:, :])
                        ins = V.tensor_tensor_scan(x_scan[:, :], x_extra[:, :], zeros[:, :], 0.0, ALU.add, ALU.add)
                    elif i == 16:
                        V.tensor_copy(x_start[:, :], x_scan[:, :])
                        ins = V.tensor_scalar(x_shift[:, :], x_scan[:, 0:C], float(1 << 13), None, ALU.mult)
                    elif i == 17:
                        ins = V.tensor_tensor(x_entry[:, :], x_shift[:, :], key_int[:, :], ALU.bitwise_or)
                    else:
                        V.sem_inc(plan_ready, 1)
                        return
                    ins.then_inc(step, 1)

                def extras(q, b):
                    count = dve.value_load(x_counti[0:1, 0:1], min_val=0, max_val=C)
                    with dve.If(count > 0):
                        with dve.Fori(0, count) as e:
                            entry = dve.value_load(x_entry[0:1, bass.ds(e, 1)], min_val=0, max_val=2 ** 30)
                            c = dve.snap(entry & (C - 1), min_val=0, max_val=C - 1)
                            deg = dve.snap((entry >> 5) & 255).with_bounds(min_val=ROUNDS + 1, max_val=P)
                            start = dve.snap(entry >> 13, min_val=0, max_val=C * TILES * P)
                            with dve.Fori(ROUNDS, deg) as k:
                                dve.wait_ge(xkept, start + k - ROUNDS + 1)
                                nc.vector.tensor_scalar(xsel[:, :], order[:, b, bass.ds(c, 1), :].rearrange("p c i -> p (c i)"),
                                                        rank_tab[:, bass.ds(k, 1)], None, ALU.is_equal).then_inc(xsel_ready, 1)
                                dve.wait_ge(xpicked, start + k - ROUNDS + 1)
                                nc.vector.tensor_tensor(acc[:, b, 0, 0:TI], extra_ps[:, :], acc[:, b, 0, 0:TI],
                                                        ALU.max).then_inc(xkept, 1)
                    dve.end_ifs()
                    total = dve.value_load(x_start[0:1, C:C + 1], min_val=0, max_val=C * TILES * P)
                    dve.wait_ge(xkept, total + 1)
                    nc.vector.sem_inc(extras_done, 1)

                def finish(q, b):
                    n[0] = PLAN
                    base = (q + 1) * (PLAN + 1) + pre
                    lk = lambda ins: link(ins, base)
                    lk(nc.vector.tensor_tensor(acc[:, b, 0, :], acc[:, b, 0, :], acc[:, b, 1, :], ALU.max))
                    nc.vector.tensor_tensor(best[:, bass.ds(q * TI, TI)], acc[:, b, 0, 0:TI], acc[:, b, 0, TI:W], ALU.max).then_inc(folded, 1)

                def tile(q, b, first):
                    if not first:
                        wait_apart(dve, acc_clear, q, passed_dve)
                    maxima(q, b, 0, STEPS // 2 - PLAN_STEPS)
                    for i in range(PLAN_STEPS):
                        step_maxima(q, b, STEPS // 2 - PLAN_STEPS + i, lambda k: plan(q, i * ROUNDS + k))
                    extras(q, 1 - b)
                    if first:
                        nc.vector.sem_inc(step, 1)
                        nc.vector.sem_inc(folded, 1)
                    else:
                        finish(q - 1, 1 - b)
                    maxima(q, b, STEPS // 2, STEPS)

                for b in range(2):
                    tile(b, b, b == 0)
                with dve.Fori(1, TILES // 2) as qq:
                    for b in range(2):
                        tile(qq * 2 + b, b, False)
                for i in range(PLAN + 1):
                    plan(TILES, i)
                extras(TILES, 1)
                finish(TILES - 1, 1)


def project(nc, x_rows, w, a, ident32, best, x1, wh, score_t, score_s):
    ctx = ExitStack()
    with ctx:
        sb = lambda name, shape, dt: ctx.enter_context(nc.sbuf_tensor(name, shape, dt))
        ps = lambda name, shape, dt: ctx.enter_context(nc.psum_tensor(name, shape, dt))
        sem = lambda name: ctx.enter_context(nc.semaphore(name))
        h = sb("h1", [P, C, D], F32)
        h_t = sb("h1_t", [P, N], F32)
        w_sb = sb("w_sb", [P, D], F32)
        w_t = sb("w_t", [P, D], F32)
        a12 = sb("a12", [P, 2], F32)
        a_wide = sb("a_wide", [P, D + 1], F32)
        wa = sb("wa", [P, D + 1], F32)
        ones = sb("ones", [P, D], F32)
        stats, mom = sb("ln2_stats", [P, C, 6], F32), sb("ln2_mom", [P, C, 2], F32)
        std, rstd, eps = sb("ln2_std", [P, C], F32), sb("ln2_rstd", [P, C], F32), sb("ln2_eps", [P, 1], F32)
        RINGB = 7
        banks = [ps(f"bank{i}", [P, 512], F32) for i in range(RINGB)]
        small_ps = ps("small_ps", [P, 512], F32)
        wt_ps, wa_ps, s_ps = small_ps[:, 0:D], small_ps[:, D:2 * D + 1], small_ps[:, 3 * D:3 * D + C]
        HALVES = 2
        GR = C // 4
        GH, CH = GR // HALVES, C // HALVES
        x_in, w_in = [sem(f"x1_in{i}") for i in range(HALVES)], sem("w_in")
        put = sem("put")
        took = sem("took")
        small_put, small_took = sem("small_put"), sem("small_took")
        x1_made, eps_made, wide_made, mom_made, std_made, h_made, step = (sem(n) for n in (
            "x1_made", "eps_made", "wide_made", "mom_made", "std_made", "h_made", "ln2_step"))
        group = lambda t, g: t[:, g * 512:(g + 1) * 512]
        with nc.Block() as block:
            @block.sync
            def _(sp):
                sp.dma_start(w_sb[:, :], w).then_inc(w_in, 16)
                sp.dma_start(a12[:, 0:1], a[0:D, :]).then_inc(w_in, 16)
                sp.dma_start(a12[:, 1:2], a[D:2 * D, :]).then_inc(w_in, 16)
                for i in range(HALVES):
                    sp.dma_start(x1[:, i * CH:(i + 1) * CH, :], x_rows[:, i * CH:(i + 1) * CH, :]).then_inc(x_in[i], 16)

            @block.tensor
            def _(pe):
                def bank(i):
                    before = i - RINGB
                    if 0 <= before < GR:
                        pe.wait_ge(x1_made, before + 1)
                    elif before >= GR:
                        pe.wait_ge(took, before - GR + 1)
                    return banks[i % RINGB]

                for g in range(GR):
                    to = bank(g)
                    for c in range(4):
                        last = nc.tensor.transpose(to[:, c * P:(c + 1) * P], best[:, (g * 4 + c) * P:(g * 4 + c + 1) * P], ident32[:, :])
                    last.then_inc(put, 1)
                    if g == 3:
                        pe.wait_ge(w_in, 48)
                        nc.tensor.transpose(wt_ps, w_sb[:, :], ident32[:, :]).then_inc(small_put, 1)
                        pe.wait_ge(small_took, 1)
                        pe.wait_ge(wide_made, 1)
                        nc.tensor.matmul(wa_ps, w_t[:, :], a_wide[:, :], start=True, stop=True).then_inc(small_put, 1)
                for g in range(GR):
                    to = bank(GR + g)
                    pe.wait_ge(h_made, g + 1)
                    for c in range(4):
                        last = nc.tensor.transpose(to[:, c * P:(c + 1) * P], h[:, g * 4 + c, :], ident32[:, :])
                    last.then_inc(put, 1)
                pe.wait_ge(small_took, 2)
                for g in range(GR):
                    to = bank(2 * GR + g)
                    pe.wait_ge(took, g + 1)
                    nc.tensor.matmul(to[:, :], wa[:, 0:D], group(h_t, g), start=True, stop=True).then_inc(put, 1)
                for c in range(C):
                    last = nc.tensor.matmul(s_ps[:, c:c + 1], h_t[:, c * P:(c + 1) * P], wa[:, D:D + 1], start=True, stop=True)
                last.then_inc(small_put, 1)
                for g in range(GR):
                    to = bank(3 * GR + g)
                    for c in range(4):
                        last = nc.tensor.matmul(to[:, c * P:(c + 1) * P], h_t[:, (g * 4 + c) * P:(g * 4 + c + 1) * P], w_sb[:, :],
                                                start=True, stop=True)
                    last.then_inc(put, 1)

            @block.scalar
            def _(act):
                act.wait_ge(small_put, 1)
                nc.scalar.activation(w_t[:, :], wt_ps, ACT.Copy).then_inc(small_took, 1)
                act.wait_ge(small_put, 2)
                nc.scalar.activation(wa[:, :], wa_ps, ACT.Copy).then_inc(small_took, 1)
                act.wait_ge(eps_made, 1)
                for i in range(HALVES):
                    act.wait_ge(mom_made, i + 1)
                    nc.scalar.activation(std[:, i * CH:(i + 1) * CH], mom[:, i * CH:(i + 1) * CH, 1], ACT.Sqrt, bias=eps[:, :]).then_inc(std_made, 1)
                for i in range(3 * GR):
                    g = i % GR
                    if i == 2 * GR:
                        act.wait_ge(small_put, 3)
                        nc.scalar.activation(score_s[:, :], s_ps, ACT.Copy)
                    act.wait_ge(put, GR + i + 1)
                    src = banks[(GR + i) % RINGB][:, :]
                    if i >= 2 * GR:
                        dst, src = wh[:, g * 4:(g + 1) * 4, 0:D], src.rearrange("p (c d) -> p c d", d=D)
                    else:
                        dst = group((h_t, score_t)[i // GR], g)
                    nc.scalar.activation(dst, src, ACT.Copy).then_inc(took, 1)

            @block.vector
            def _(dve):
                n = [0]

                def link(ins):
                    n[0] += 1
                    ins.then_inc(step, 1)
                    dve.wait_ge(step, n[0])

                def moments(i):
                    dve.wait_ge(x_in[i], 16)
                    for g in range(i * GH, (i + 1) * GH):
                        dve.wait_ge(put, g + 1)
                        xg = x1[:, g * 4:(g + 1) * 4, :].rearrange("p c d -> p (c d)")
                        nc.vector.scalar_tensor_tensor(out=xg, in0=banks[g % RINGB][:, :], scalar=1.0 / HSCALE, in1=xg,
                                                       op0=ALU.mult, op1=ALU.add).then_inc(x1_made, 1)
                    dve.wait_ge(x1_made, (i + 1) * GH)
                    for c in range(i * CH, (i + 1) * CH):
                        last = nc.vector.bn_stats(stats[:, c, :], x1[:, c, :])
                    link(last)
                    for c in range(i * CH, (i + 1) * CH):
                        last = nc.vector.bn_aggr(mom[:, c, :], stats[:, c, :])
                    last.then_inc(mom_made, 1)

                def normalise(i):
                    s_, r_ = std[:, i * CH:(i + 1) * CH], rstd[:, i * CH:(i + 1) * CH]
                    dve.wait_ge(std_made, i + 1)
                    link(nc.vector.reciprocal(r_, s_))
                    link(nc.vector.tensor_tensor(s_, r_, r_, ALU.mult))
                    link(nc.vector.scalar_tensor_tensor(out=s_, in0=mom[:, i * CH:(i + 1) * CH, 1], scalar=eps[:, :], in1=s_,
                                                        op0=ALU.add, op1=ALU.mult))
                    link(nc.vector.tensor_scalar(s_, s_, -0.5, 1.5, ALU.mult, ALU.add))
                    link(nc.vector.tensor_tensor(r_, r_, s_, ALU.mult))
                    for g in range(i * GH, (i + 1) * GH):
                        for c in range(g * 4, g * 4 + 4):
                            last = nc.vector.tensor_scalar(h[:, c, :], x1[:, c, :], mom[:, c, 0:1], rstd[:, c:c + 1], ALU.subtract, ALU.mult)
                        link(last)
                        hg = h[:, g * 4:(g + 1) * 4, :]
                        nc.vector.tensor_scalar(hg, hg, 0.0, None, ALU.max).then_inc(h_made, 1)

                nc.vector.memset(eps[:, :], EPS).then_inc(eps_made, 1)
                nc.vector.memset(wh[:, :, D:D + 1], 1.0)
                link(nc.vector.memset(ones[:, :], 1.0))
                dve.wait_ge(w_in, 48)
                nc.vector.tensor_copy(a_wide[:, D:D + 1], a12[:, 0:1])
                nc.vector.tensor_scalar(a_wide[:, 0:D], ones[:, :], a12[:, 1:2], None, ALU.mult).then_inc(wide_made, 1)
                for i in range(HALVES):
                    moments(i)
                    normalise(i)


def attend(nc, absent_rows, out_rows, ident32, x1, wh, score_t, score_s):
    ctx = ExitStack()
    with ctx:
        sb = lambda name, shape, dt: ctx.enter_context(nc.sbuf_tensor(name, shape, dt))
        sem = lambda name: ctx.enter_context(nc.semaphore(name))
        RING = 4
        GR = C // 4
        PARTS = 4
        PW = N // PARTS
        OUTER = N // P // RING
        y = sb("y", [P, RING, N], F32)
        gone = sb("gone", [P, 2, N], BF16)
        turned = sb("turned", [P, 4, 512], F32)
        z = sb("z", [P, 2, N], F32)
        top = sb("top", [P, RING, PARTS], F32)
        row = sb("row", [P, RING, 8], F32)
        rden = sb("rden", [P, RING], F32)
        att = sb("att", [P, 2, RING, D], F32)
        low = sb("low", [P, 2, RING, D], F32)
        turn_ps = [ctx.enter_context(nc.psum_tensor(f"turn_ps{i}", [P, 512], F32)) for i in range(4)]
        out_ps = [ctx.enter_context(nc.psum_tensor(f"out_ps{i}", [P, D + 1], F32)) for i in range(2)]
        gone_in = [sem(f"gone_in{i}") for i in range(2)]
        scored = sem("scored")
        row_step = sem("row_step")
        biased = sem("biased")
        weighed = sem("weighed")
        blended = sem("blended")
        turned_g = sem("turned_g")
        moved_a, moved_v = sem("moved_a"), sem("moved_v")
        mixed = sem("mixed")
        rden_made = sem("rden_made")
        normed = sem("normed")
        low_made, low_exp, fin_step = sem("low_made"), sem("low_exp"), sem("fin_step")
        att_free, low_free, finished = sem("att_free"), sem("low_free"), sem("finished")
        stored = sem("stored")
        passed_p, passed_a, passed_v, passed_sp = (sem("passed_" + e) for e in "pavs")
        BY_ACT = (0, 1, 2, 4, 5, 6)
        BY_DVE = (3, 7)
        NA, NV = len(BY_ACT), len(BY_DVE)

        def all_tiles(eng, tiles):
            tiles(0, 0, True, False)
            with eng.Fori(0, OUTER // 2 - 1) as oo:
                tiles(oo * 2 + 1, 1, False, False)
                tiles(oo * 2 + 2, 0, False, False)
            tiles(OUTER - 1, 1, False, True)

        with nc.Block() as block:
            @block.sync
            def _(sp):
                def load(r, slot):
                    sp.dma_start(gone[:, slot, :], absent_rows[bass.ds(r * P, P), :]).then_inc(gone_in[slot], 16)

                def store(o, k):
                    wait_apart(sp, finished, o + 1, passed_sp)
                    sp.dma_start(out_rows[:, bass.ds(o * RING, RING), :], low[:, k, :, :]).then_inc(stored, 16)
                    wait_apart(sp, stored, (o + 1) * 16, passed_sp)
                    sp.sem_inc(low_free, 1)

                def tiles(o, k, first, last):
                    for b in range(RING):
                        if not (last and b >= RING - 2):
                            wait_apart(sp, scored, (o * RING + b + 1) * PARTS, passed_sp)
                            load(o * RING + b + 2, b % 2)
                        if b == 2 and not first:
                            store(o - 1, 1 - k)

                sp.sem_inc(low_free, 2)
                load(0, 0)
                load(1, 1)
                all_tiles(sp, tiles)
                store(OUTER - 1, 1)

            @block.vector
            def _(dve):
                def score(o, b, part):
                    if part == 0:
                        wait_apart(dve, gone_in[b % 2], 16 * (o * (RING // 2) + b // 2 + 1), passed_v)
                    nc.vector.tensor_tensor_reduce(out=y[:, b % RING, part * PW:(part + 1) * PW],
                                                   in0=score_t[:, part * PW:(part + 1) * PW],
                                                   in1=gone[:, b % 2, part * PW:(part + 1) * PW],
                                                   scale=1.0, scalar=-3e38, op0=ALU.subtract, op1=ALU.max,
                                                   accum_out=top[:, b % RING, part:part + 1]).then_inc(scored, 1)

                def blend(o, b, part):
                    yy = y[:, b % RING, part * PW:(part + 1) * PW]
                    dve.wait_ge(weighed, PARTS * (o * RING + b) + part + 1)
                    nc.vector.tensor_tensor(yy, yy, z[:, b % 2, part * PW:(part + 1) * PW], ALU.max).then_inc(blended, 1)

                def move(r, i):
                    g = BY_DVE[i]
                    dve.wait_ge(turned_g, (r + 2) * GR + g + 1)
                    dve.wait_ge(mixed, r * GR + g + 1)
                    nc.vector.tensor_copy(turned[:, g % 4, :], turn_ps[g % 4][:, :]).then_inc(moved_v, 1)

                def norm(o, b, k):
                    r = o * RING + b
                    if b == 0:
                        dve.wait_ge(att_free, o + 1)
                    dve.wait_ge(mixed, (r + 1) * GR + 4)
                    nc.vector.reciprocal(rden[:, b:b + 1], out_ps[b % 2][:, D:D + 1]).then_inc(rden_made, 1)
                    dve.wait_ge(rden_made, r + 1)
                    nc.vector.tensor_scalar(att[:, k, b, :], out_ps[b % 2][:, 0:D], rden[:, b:b + 1], None, ALU.mult).then_inc(normed, 1)

                def tiles(o, k, first, last):
                    for b in range(RING):
                        r = o * RING + b
                        for what, i in (("blend", 0), ("score", 0), ("blend", 1), ("move", 0), ("norm", 0), ("score", 1), ("blend", 2),
                                        ("score", 2), ("blend", 3), ("move", 1), ("score", 3)):
                            if what == "blend" and not (last and b == RING - 1):
                                blend(o, b + 1, i)
                            elif what == "score" and not (last and b >= RING - 3):
                                if i == 0:
                                    dve.wait_ge(turned_g, (r + 2) * GR)
                                score(o, b + 3, i)
                            elif what == "move":
                                move(r, i)
                            elif what == "norm" and not (first and b == 0):
                                norm(o if b else o - 1, b - 1 if b else RING - 1, k if b else 1 - k)

                dve.sem_inc(att_free, 2)
                dve.sem_inc(moved_v, NV)
                dve.sem_inc(normed, 2)
                for b in range(3):
                    for part in range(PARTS):
                        score(0, b, part)
                for part in range(PARTS):
                    blend(0, 0, part)
                all_tiles(dve, tiles)
                norm(OUTER - 1, RING - 1, 1)

            @block.scalar
            def _(act):
                def weigh(o, b, part, second):
                    r, yy, zz = o * RING + b, y[:, b % RING, part * PW:(part + 1) * PW], z[:, b % 2, part * PW:(part + 1) * PW]
                    if not second:
                        act.wait_ge(biased, 2 * r + 2)
                        act.wait_ge(blended, PARTS * r + part + 1)
                        nc.scalar.activation(zz, yy, ACT.Exp, scale=ALPHA, bias=row[:, b % RING, 4:5])
                    else:
                        nc.scalar.activation(yy, yy, ACT.Exp, bias=row[:, b % RING, 3:4]).then_inc(weighed, 1)

                def move(r, i):
                    g = BY_ACT[i]
                    act.wait_ge(turned_g, (r + 2) * GR + g + 1)
                    act.wait_ge(mixed, r * GR + g + 1)
                    nc.scalar.activation(turned[:, g % 4, :], turn_ps[g % 4][:, :], ACT.Copy).then_inc(moved_a, 1)

                def exp_low(o, k):
                    act.wait_ge(low_made, o + 1)
                    nc.scalar.activation(low[:, k, :, :], low[:, k, :, :], ACT.Exp).then_inc(low_exp, 1)

                def tiles(o, k, first, last):
                    for b in range(RING):
                        r = o * RING + b
                        ahead = not (last and b >= RING - 2)
                        for it in ((0, 0), 0, (0, 1), 1, (1, 0), 2, (1, 1), (2, 0), 3, (2, 1), 4, (3, 0), 5, (3, 1)):
                            if isinstance(it, int):
                                move(r, it)
                            elif ahead:
                                weigh(o, b + 2, *it)
                        if b == 0 and not first:
                            exp_low(o - 1, 1 - k)

                act.sem_inc(blended, 2 * PARTS)
                act.sem_inc(moved_a, NA)
                for b in range(2):
                    for part in range(PARTS):
                        weigh(0, b, part, 0)
                        weigh(0, b, part, 1)
                all_tiles(act, tiles)
                exp_low(OUTER - 1, 1)

            @block.tensor
            def _(pe):
                def wait_moved(r, g):
                    if g in BY_ACT:
                        pe.wait_ge(moved_a, (r + 1) * NA + BY_ACT.index(g) + 1)
                    else:
                        pe.wait_ge(moved_v, (r + 1) * NV + BY_DVE.index(g) + 1)

                def turn(r, b, g):
                    r, b, g = r + g // GR, b + g // GR, g % GR
                    pe.wait_ge(blended, PARTS * (r + 2) + g // (GR // PARTS) + 1)
                    wait_moved(r if g >= 4 else r - 1, (g - 4) % GR)
                    for c in range(4):
                        last = nc.tensor.transpose(turn_ps[g % 4][:, c * P:(c + 1) * P], y[:, b % RING, (g * 4 + c) * P:(g * 4 + c + 1) * P],
                                                   ident32[:, :])
                    last.then_inc(turned_g, 1)

                def mix(r, b, g):
                    wait_moved(r, g)
                    if g == 0:
                        pe.wait_ge(normed, r + 1)
                    for c in range(4):
                        last = nc.tensor.matmul(out_ps[b % 2][:, :], turned[:, g % 4, c * P:(c + 1) * P], wh[:, g * 4 + c, :],
                                                start=g == 0 and c == 0, stop=g == GR - 1 and c == 3)
                    last.then_inc(mixed, 1)

                def tiles(o, k, first, last):
                    for b in range(RING):
                        for g in range(GR):
                            if not (last and b == RING - 1 and g + 3 >= GR):
                                turn(o * RING + b, b, g + 3)
                            mix(o * RING + b, b, g)

                pe.sem_inc(turned_g, 2 * GR)
                pe.sem_inc(mixed, 4)
                for g in range(3):
                    turn(0, 0, g)
                all_tiles(pe, tiles)

            @block.gpsimd
            def _(pool):
                def cut(o, k):
                    pool.wait_ge(low_free, o + 1)
                    wait_apart(pool, normed, (o + 1) * RING + 2, passed_p)
                    nc.gpsimd.tensor_scalar(low[:, k, :, :], att[:, k, :, :], 0.0, None, ALU.min).then_inc(low_made, 1)
                    nc.gpsimd.tensor_scalar(att[:, k, :, :], att[:, k, :, :], 0.0, -1.0, ALU.max, ALU.add).then_inc(fin_step, 1)
                    wait_apart(pool, fin_step, 2 * o + 1, passed_p)
                    nc.gpsimd.tensor_tensor(att[:, k, :, :], att[:, k, :, :], x1[:, bass.ds(o * RING, RING), :], ALU.add).then_inc(fin_step, 1)

                def finish(o, k):
                    wait_apart(pool, fin_step, 2 * o + 2, passed_p)
                    wait_apart(pool, low_exp, o + 1, passed_p)
                    nc.gpsimd.tensor_tensor(low[:, k, :, :], low[:, k, :, :], att[:, k, :, :], ALU.add).then_inc(finished, 1)
                    pool.wait_ge(finished, o + 1)
                    pool.sem_inc(att_free, 1)

                def bias(o, b):
                    r, at = o * RING + b, b % RING
                    col = lambda i: row[:, at, i:i + 1]
                    n = [0]

                    def step(ins):
                        n[0] += 1
                        ins.then_inc(row_step, 1)
                        wait_apart(pool, row_step, r * 4 + n[0], passed_p)

                    step(nc.gpsimd.tensor_copy(col(0), score_s[:, bass.ds(r, 1)]))
                    wait_apart(pool, scored, PARTS * (r + 1), passed_p)
                    step(nc.gpsimd.tensor_scalar(col(5), top[:, at, 0:1], top[:, at, 1:2], top[:, at, 2:3], ALU.max, ALU.max))
                    step(nc.gpsimd.tensor_scalar(col(1), col(5), top[:, at, 3:4], col(0), ALU.max, ALU.add))
                    step(nc.gpsimd.tensor_scalar(col(2), col(1), ALPHA, col(1), ALU.mult, ALU.max))
                    nc.gpsimd.tensor_scalar(col(3), col(0), col(2), None, ALU.subtract).then_inc(biased, 1)
                    nc.gpsimd.tensor_scalar(col(4), col(0), ALPHA, col(2), ALU.mult, ALU.subtract).then_inc(biased, 1)

                def tiles(o, k, first, last):
                    for b in range(RING):
                        bias(o, b)
                        if b == 2 and not first:
                            cut(o - 1, 1 - k)
                        if b == 3 and not first:
                            finish(o - 1, 1 - k)

                all_tiles(pool, tiles)
                cut(OUTER - 1, 1)
                finish(OUTER - 1, 1)


def kernel(x, adj, L1_gnn_W, L1_gnn_a):
    import numpy as np
    import concourse.bacc as bacc
    from concourse.bass_utils import run_bass_kernel_spmd as run
    nc = bacc.Bacc("TRN2", target_bir_lowering=False, num_devices=1)
    arrays, args = {}, []
    for name, arr in (("x", x), ("adj", adj), ("w", L1_gnn_W), ("a", L1_gnn_a)):
        arr = np.ascontiguousarray(arr)
        arrays[name] = arr
        args.append(nc.dram_tensor(name, arr.shape, mybir.dt.from_np(arr.dtype), kind="ExternalInput").ap())
    out = nc.dram_tensor("out", (N, D), F32, kind="ExternalOutput").ap()
    gnn_two_layers(nc, *args, out)
    result = run(nc, [arrays], core_ids=[0])
    return result.results[0]["out"]
```
